# Optimizing a Trainium2 kernel written in Bass

```python
import numpy as np
import jax
import jax.numpy as jnp

def _softmax(x, axis=-1):
    return jax.nn.softmax(x, axis=axis)

def _gelu(x):
    return jax.nn.gelu(x, approximate=True)

def _silu(x):
    return jax.nn.silu(x)

def _sigmoid(x):
    return jax.nn.sigmoid(x)

def _layernorm(x, axis=-1, eps=1e-05):
    m = jnp.mean(x, axis=axis, keepdims=True)
    v = jnp.var(x, axis=axis, keepdims=True)
    return (x - m) / jnp.sqrt(v + eps)

def _scatter_add(tgt, idx, src, axis=0):
    return tgt.at[idx].add(src)

def _segment_sum(src, seg, n):
    return jax.ops.segment_sum(src, seg, n)
kernel_name = 'mk_hybrid_d1_jaxref_r8_25d5ce'

def setup_inputs(seed: int=0):
    np.random.seed(seed)
    _w = jnp.asarray

    def _L0_attn_a_setup():
        import jax, jax.numpy as jnp
        import numpy as np
        DIM = 128
        NUM_HEADS = 16
        NUM_GROUPS = 8

        def grouped_linear(x, w, b):
            B, N, Cin = x.shape
            G = w.shape[0]
            xg = x.reshape(B, N, G, Cin // G)
            out = jnp.einsum('bngi,gio->bngo', xg, w)
            out = out.reshape(B, N, -1)
            if b is not None:
                out = out + b
            return out
        key = jax.random.key(seed)
        k1, k2, k3, k4 = jax.random.split(key, 4)
        G = NUM_GROUPS
        x = jax.random.normal(k1, (2, 256, DIM), dtype=jnp.float32)
        w_qkv = jax.random.normal(k2, (G, DIM // G, 3 * DIM // G), dtype=jnp.float32) * (DIM // G) ** (-0.5)
        w_proj = jax.random.normal(k3, (G, DIM // G, DIM // G), dtype=jnp.float32) * (DIM // G) ** (-0.5)
        b_proj = jax.random.normal(k4, (DIM,), dtype=jnp.float32) * 0.02
        return {'x': x, 'w_qkv': w_qkv, 'w_proj': w_proj, 'b_proj': b_proj}
    _L0_attn_a_in = _L0_attn_a_setup()

    def _L0_attn_b_setup():
        import jax, jax.numpy as jnp
        import numpy as np
        N_HEAD = 16
        BUCKET = 64
        HIDDEN = 128
        EPS = 1e-05

        def _ln(x, g, b):
            m = x.mean(-1, keepdims=True)
            v = x.var(-1, keepdims=True)
            return (x - m) * jax.lax.rsqrt(v + EPS) * g + b
        key = jax.random.key(seed)
        ks = jax.random.split(key, 6)

        def w(k, shape, s=0.02):
            return jax.random.normal(k, shape, jnp.float32) * s
        C = HIDDEN
        return {'x': jax.random.normal(ks[0], (4, 1024, C), jnp.float32), 'ln1_g': jnp.ones((C,), jnp.float32), 'ln1_b': jnp.zeros((C,), jnp.float32), 'w_qkv': w(ks[1], (C, 3 * C)), 'b_qkv': jnp.zeros((3 * C,), jnp.float32), 'w_out': w(ks[2], (C, C)), 'b_out': jnp.zeros((C,), jnp.float32), 'ln2_g': jnp.ones((C,), jnp.float32), 'ln2_b': jnp.zeros((C,), jnp.float32), 'w1': w(ks[3], (C, 4 * C)), 'b1': jnp.zeros((4 * C,), jnp.float32), 'w2': w(ks[4], (4 * C, C)), 'b2': jnp.zeros((C,), jnp.float32)}
    _L0_attn_b_in = _L0_attn_b_setup()

    def _L0_ffn_setup():
        import jax, jax.numpy as jnp
        import numpy as np
        H = 128
        E = 8
        FFN = 512
        TOP_K = 2
        key = jax.random.key(seed)
        ks = jax.random.split(key, 6)
        s_h = 1.0 / np.sqrt(H)
        s_f = 1.0 / np.sqrt(FFN)
        return {'hidden_states': jax.random.normal(ks[0], (4, 128, H), dtype=jnp.float32), 'router_w': jax.random.uniform(ks[1], (E, H), jnp.float32, -s_h, s_h), 'w1': jax.random.uniform(ks[2], (E, FFN, H), jnp.float32, -s_h, s_h), 'b1': jax.random.uniform(ks[3], (E, FFN), jnp.float32, -s_h, s_h), 'w2': jax.random.uniform(ks[4], (E, H, FFN), jnp.float32, -s_f, s_f), 'b2': jax.random.uniform(ks[5], (E, H), jnp.float32, -s_f, s_f)}
    _L0_ffn_in = _L0_ffn_setup()
    _d = {'L0_attn_a_x': _L0_attn_a_in['x'], 'L0_attn_a_w_qkv': _L0_attn_a_in['w_qkv'], 'L0_attn_a_w_proj': _L0_attn_a_in['w_proj'], 'L0_attn_a_b_proj': _L0_attn_a_in['b_proj'], 'L0_attn_b_ln1_g': _L0_attn_b_in['ln1_g'], 'L0_attn_b_ln1_b': _L0_attn_b_in['ln1_b'], 'L0_attn_b_w_qkv': _L0_attn_b_in['w_qkv'], 'L0_attn_b_b_qkv': _L0_attn_b_in['b_qkv'], 'L0_attn_b_w_out': _L0_attn_b_in['w_out'], 'L0_attn_b_b_out': _L0_attn_b_in['b_out'], 'L0_attn_b_ln2_g': _L0_attn_b_in['ln2_g'], 'L0_attn_b_ln2_b': _L0_attn_b_in['ln2_b'], 'L0_attn_b_w1': _L0_attn_b_in['w1'], 'L0_attn_b_b1': _L0_attn_b_in['b1'], 'L0_attn_b_w2': _L0_attn_b_in['w2'], 'L0_attn_b_b2': _L0_attn_b_in['b2'], 'L0_ffn_router_w': _L0_ffn_in['router_w'], 'L0_ffn_w1': _L0_ffn_in['w1'], 'L0_ffn_b1': _L0_ffn_in['b1'], 'L0_ffn_w2': _L0_ffn_in['w2'], 'L0_ffn_b2': _L0_ffn_in['b2']}
    _x0 = _d['L0_attn_a_x']
    _d['L0_attn_a_x'] = jax.random.normal(jax.random.fold_in(jax.random.key(seed), 1), (2, 1024, 128), dtype=_x0.dtype)
    del _x0
    return _d

def reference(L0_attn_a_x, L0_attn_a_w_qkv, L0_attn_a_w_proj, L0_attn_a_b_proj, L0_attn_b_ln1_g, L0_attn_b_ln1_b, L0_attn_b_w_qkv, L0_attn_b_b_qkv, L0_attn_b_w_out, L0_attn_b_b_out, L0_attn_b_ln2_g, L0_attn_b_ln2_b, L0_attn_b_w1, L0_attn_b_b1, L0_attn_b_w2, L0_attn_b_b2, L0_ffn_router_w, L0_ffn_w1, L0_ffn_b1, L0_ffn_w2, L0_ffn_b2):

    def _L0_attn_a_ref(x, w_qkv, w_proj, b_proj):
        import jax, jax.numpy as jnp
        import numpy as np
        DIM = 128
        NUM_HEADS = 16
        NUM_GROUPS = 8

        def grouped_linear(x, w, b):
            B, N, Cin = x.shape
            G = w.shape[0]
            xg = x.reshape(B, N, G, Cin // G)
            out = jnp.einsum('bngi,gio->bngo', xg, w)
            out = out.reshape(B, N, -1)
            if b is not None:
                out = out + b
            return out
        B, N, C = x.shape
        H = NUM_HEADS
        D = C // H
        scale = D ** (-0.5)
        qkv = grouped_linear(x, w_qkv, None)
        qkv = qkv.reshape(B, N, 3, H, D)
        qkv = jnp.transpose(qkv, (2, 0, 3, 1, 4))
        q, k, v = (qkv[0] * scale, qkv[1], qkv[2])
        attn = jnp.einsum('bhnd,bhmd->bhnm', q, k)
        attn = jax.nn.softmax(attn, axis=-1)
        out = jnp.einsum('bhnm,bhmd->bhnd', attn, v)
        out = jnp.transpose(out, (0, 2, 1, 3)).reshape(B, N, C)
        out = grouped_linear(out, w_proj, b_proj)
        return out

    def _L0_attn_b_ref(x, ln1_g, ln1_b, w_qkv, b_qkv, w_out, b_out, ln2_g, ln2_b, w1, b1, w2, b2):
        import jax, jax.numpy as jnp
        import numpy as np
        N_HEAD = 16
        BUCKET = 64
        HIDDEN = 128
        EPS = 1e-05

        def _ln(x, g, b):
            m = x.mean(-1, keepdims=True)
            v = x.var(-1, keepdims=True)
            return (x - m) * jax.lax.rsqrt(v + EPS) * g + b
        B, T, C = x.shape
        nb = T // BUCKET
        hd = C // N_HEAD
        scale = 1.0 / np.sqrt(hd)
        h = _ln(x, ln1_g, ln1_b)
        qkv = h @ w_qkv + b_qkv
        q, k, v = jnp.split(qkv, 3, axis=-1)

        def buck(t):
            return t.reshape(B, nb, BUCKET, N_HEAD, hd)
        qb, kb, vb = (buck(q), buck(k), buck(v))
        kp = jnp.concatenate([jnp.zeros_like(kb[:, :1]), kb[:, :-1]], axis=1)
        vp = jnp.concatenate([jnp.zeros_like(vb[:, :1]), vb[:, :-1]], axis=1)
        kc = jnp.concatenate([kp, kb], axis=2)
        vc = jnp.concatenate([vp, vb], axis=2)
        scores = jnp.einsum('bnihd,bnjhd->bnhij', qb, kc) * scale
        i = jnp.arange(BUCKET)[:, None]
        j = jnp.arange(2 * BUCKET)[None, :]
        mask = (j < BUCKET) | (j - BUCKET <= i)
        scores = jnp.where(mask, scores, -jnp.inf)
        attn = jax.nn.softmax(scores, axis=-1)
        ob = jnp.einsum('bnhij,bnjhd->bnihd', attn, vc).reshape(B, T, C)
        x = x + ob @ w_out + b_out
        h2 = _ln(x, ln2_g, ln2_b)
        m = jax.nn.gelu(h2 @ w1 + b1, approximate=False) @ w2 + b2
        return x + m

    def _L0_ffn_ref(hidden_states, router_w, w1, b1, w2, b2):
        import jax, jax.numpy as jnp
        import numpy as np
        H = 128
        E = 8
        FFN = 512
        TOP_K = 2
        B, S, _ = hidden_states.shape
        x = hidden_states.reshape(-1, H)
        T = x.shape[0]
        logits = x @ router_w.T
        top_v, top_i = jax.lax.top_k(logits, TOP_K)
        rw = jax.nn.softmax(top_v, axis=-1)
        combine = jnp.zeros((T, E), x.dtype).at[jnp.arange(T)[:, None], top_i].add(rw)
        h = jax.nn.gelu(jnp.einsum('th,efh->etf', x, w1) + b1[:, None, :], approximate=False)
        y = jnp.einsum('etf,ehf->eth', h, w2) + b2[:, None, :]
        out = jnp.einsum('eth,te->th', y, combine)
        return out.reshape(B, S, H)
    x = L0_attn_a_x
    x = x + _L0_attn_a_ref(_layernorm(x, axis=-1), L0_attn_a_w_qkv, L0_attn_a_w_proj, L0_attn_a_b_proj)
    x = x + _L0_ffn_ref(_layernorm(x, axis=-1), L0_ffn_router_w, L0_ffn_w1, L0_ffn_b1, L0_ffn_w2, L0_ffn_b2)
    x = x + _L0_attn_b_ref(_layernorm(x, axis=-1), L0_attn_b_ln1_g, L0_attn_b_ln1_b, L0_attn_b_w_qkv, L0_attn_b_b_qkv, L0_attn_b_w_out, L0_attn_b_b_out, L0_attn_b_ln2_g, L0_attn_b_ln2_b, L0_attn_b_w1, L0_attn_b_b1, L0_attn_b_w2, L0_attn_b_b2)
    x = x + _L0_ffn_ref(_layernorm(x, axis=-1), L0_ffn_router_w, L0_ffn_w1, L0_ffn_b1, L0_ffn_w2, L0_ffn_b2)
    return x

_drawn_inputs = setup_inputs


def setup_inputs(seed=0):
    import zlib

    import numpy as np

    out = dict(_drawn_inputs(seed))
    spreads = {'L0_attn_b_ln1_g': (1.0, 0.6),
     'L0_attn_b_ln1_b': (0.0, 0.8),
     'L0_attn_b_b_qkv': (0.0, 0.627),
     'L0_attn_b_b_out': (0.0, 0.1),
     'L0_attn_b_ln2_g': (1.0, 0.6),
     'L0_attn_b_ln2_b': (0.0, 2.0),
     'L0_attn_b_b1': (0.0, 0.535),
     'L0_attn_b_b2': (0.0, 0.1)}
    factors = {'L0_attn_b_w_qkv': 8.0, 'L0_attn_b_w_out': 4.213, 'L0_ffn_b1': 2.826}
    for name, (base, spread) in spreads.items():
        noise = np.random.default_rng([zlib.crc32(name.encode()), seed]).standard_normal(out[name].shape)
        drawn = base * np.exp(spread * noise) if base else spread * noise
        out[name] = jnp.asarray(drawn.astype(out[name].dtype))
    for name, factor in factors.items():
        out[name] = (out[name] * factor).astype(out[name].dtype)
    return out
```

```python
from contextlib import ExitStack

import concourse.bass as bass
from concourse import mybir

F32 = mybir.dt.float32
BF16 = mybir.dt.bfloat16
ALU = mybir.AluOpType
ACT = mybir.ActivationFunctionType
AX = mybir.AxisListType.X

P = 128
B = 2
N = 1024
T = B * N
NT = T // P
NQ = 4
QW = T // NQ
H = 16
D = P // H
HQ = 4
QUADS = H // HQ
SCALE = float(D) ** -0.5
EPS = 1e-5
K_PARTS = (0, 0, 0, 1, 1, 2)
Q_PARTS = (0, 1, 2, 0, 1, 0)
NR = len(K_PARTS)
KR = NR * D
MT = N // P
UNITS = 2 * MT
ITEMS = 34
E = 8
FF = 512
FC = FF // P
BK = 64
PADN = N + BK
VW = D + 1
PLAN = (0, 1, 2, 2, 3, 2, 3, 2, 3, 2, 3, 2, 3, 2, 2, 2)
assert sum(PLAN) == ITEMS


def max_items():
    halves = [[("max", nh, h, nt) for nt in range(4) for h in range(HQ)] for nh in range(2)]
    return halves[0] + halves[1][:2] + [("turn", 0)] + halves[1][2:] + [("turn", 1)]


ITEM_LIST = max_items()
assert len(ITEM_LIST) == ITEMS
LAST_MAX = {0: 15, 1: 32}
TURN_AT = {0: 18, 1: 33}


def build(nc, dram, out):
    with ExitStack() as ctx:
        def sb(name, shape, dt=F32):
            return ctx.enter_context(nc.sbuf_tensor(name, shape, dt))

        def scratch(name, shape, dt):
            return nc.dram_tensor(name, shape, dt, kind="Internal").ap()

        sems = {}

        def S(name):
            if name not in sems:
                sems[name] = ctx.enter_context(nc.semaphore(name))
            return sems[name]

        X = sb("X", [P, NT, P])
        XN = sb("XN", [P, NT, P])
        HN = sb("HN", [P, NT, P])
        XT = sb("XT", [P, T])
        QF = sb("QF", [P, T])
        KF = sb("KF", [P, T])
        parts = sb("parts", [P, 3, T], BF16)
        KA = [sb(f"KA{b}", [P, 2, N], BF16) for b in range(B)]
        QZ = [sb(f"QZ{b}", [P, 2, 2, N], BF16) for b in range(B)]
        PE_ = [sb(f"PE{j}", [P, HQ, 512]) for j in range(2)]
        OT = sb("OT", [P, QUADS, T])
        Vn = sb("Vn", [P, QUADS * B, MT, HQ * D])
        Vs = [sb(f"Vs{b}", [P, MT, HQ, 32]) for b in range(B)]
        mx = [sb(f"mx{j}", [P, 16]) for j in range(2)]
        neg = [sb(f"neg{j}", [16, P]) for j in range(2)]
        nres = sb("nres", [16, P])
        mparts = [sb(f"mparts{j}", [16, 3, P], BF16) for j in range(2)]
        rden = sb("rden", [P, 2, 512])
        st = sb("st", [P, NT, 6])
        mv = sb("mv", [P, NT, 2])
        rstd = sb("rstd", [P, NT])
        mhalf = sb("mhalf", [P, NT])
        ident = sb("ident", [P, P])
        identb = sb("identb", [P, P], BF16)
        sel = sb("sel", [P, P])
        causal = sb("causal", [P, P], BF16)
        wqkva = sb("wqkva", [P, 3 * P])
        wpa = sb("wpa", [P, QUADS, P])
        bpa = sb("bpa", [P, P])
        wqkvb = sb("wqkvb", [P, 3 * P])
        colb = sb("colb", [P, 12])
        bvb = sb("bvb", [P, P])
        bob = sb("bob", [P, P])
        b2b = sb("b2b", [P, P])
        wob = sb("wob", [P, P])
        w1b = sb("w1b", [P, FF])
        w2b = sb("w2b", [P, FC, P])
        rw = sb("rw", [P, E])
        b1e = sb("b1e", [P, E, FC])
        b1s = sb("b1s", [P, 2, FC])
        b2e = sb("b2e", [E, P])
        tri = sb("tri", [P, E, E])
        L = sb("L", [P, NT, E])
        beats = sb("beats", [P, NT, E, E])
        ties = sb("ties", [P, NT, E, E])
        rank = sb("rank", [P, NT, E])
        lmax = sb("lmax", [P, NT])
        comb = sb("comb", [P, NT, E])
        cw = sb("cw", [P, 2, NT])
        W1s = [KA[0][:, :, :].rearrange("p a n -> p (a n)").bitcast(F32)[:, 0:FF],
               KA[0][:, :, :].rearrange("p a n -> p (a n)").bitcast(F32)[:, FF:2 * FF]]
        W2s = [KA[1][:, :, :].rearrange("p a n -> p (a n)").bitcast(F32)[:, 0:FF].rearrange("p (f c) -> p f c", f=FC),
               KA[1][:, :, :].rearrange("p a n -> p (a n)").bitcast(F32)[:, FF:2 * FF].rearrange("p (f c) -> p f c", f=FC)]
        combT = OT[0:E, 3, :]
        V9 = OT[:, 0:2, :].rearrange("p q n -> p (q n)")[:, 0:NT * H * VW].rearrange("p (t h c) -> p t h c", t=NT, h=H)
        QB = [QZ[j][:, 0, :, :].rearrange("p a n -> p (a n)").rearrange("p (h n) -> p h n", h=H) for j in range(2)]
        KB = [QZ[j][:, 1, :, :].rearrange("p a n -> p (a n)").rearrange("p (h n) -> p h n", h=H) for j in range(2)]
        KBx = [KA[j][:, :, :].rearrange("p a n -> p (a n)")[:, 0:H * BK].rearrange("p (h n) -> p h n", h=H) for j in range(2)]
        VWs = [Vs[j][:, :, :, :].rearrange("p a h c -> p (a h c)")[:, 0:2 * H * VW].rearrange("p (w c) -> p w c", w=2) for j in range(2)]
        PB = OT[:, 2, :].rearrange("p (h n) -> p h n", h=H)
        PT = OT[:, 3, :].rearrange("p (h n) -> p h n", h=H)
        AO = QF[:, :].rearrange("p (t h d) -> p t h d", t=NT, h=H)
        mxb = sb("mxb", [P, H])
        rsb = sb("rsb", [P, H])
        zer = sb("zer", [P, 256], BF16)
        zerf = sb("zerf", [BK, H * VW])

        ps = ctx.enter_context(nc.psum_tensor("ps", [P, 8, 512], F32))
        SB, OB, MB = (0, 1, 2), 3, (4, 6)

        kst = scratch("kst", (H, KR, T), BF16)
        qst = scratch("qst", (H, KR, T), BF16)
        mrow = scratch("mrow", (B, 2, 3, 16, P), BF16)
        kstb = scratch("kstb", (H, KR, B * PADN), BF16)
        qstb = scratch("qstb", (H, KR, T), BF16)
        vst = scratch("vst", (B, PADN, H * VW), F32)

        kst_q = kst.rearrange("(q a j) r t -> q j r a t", a=2, j=2)
        qst_q = qst.rearrange("(q a j) r t -> q j r a t", a=2, j=2)

        LN1G, LN1B, LN2G, LN2B, BQ, BKC, B1C = 0, 1, 2, 3, 4, 5, 6

        block = ctx.enter_context(nc.Block())

        def hold(eng, sem, value):
            eng.wait_ge(sem, value)
            eng.nop(nofuse=True)

        def norm_vector(ve, tag, src, dst):
            for t in range(NT):
                nc.vector.bn_stats(st[:, t, :], src[:, t, :]).then_inc(S(f"{tag}_stats"), 1)
            ve.wait_ge(S(f"{tag}_stats"), NT)
            for t in range(NT):
                nc.vector.bn_aggr(mv[:, t, :], st[:, t, :]).then_inc(S(f"{tag}_moments"), 1)
            ve.wait_ge(S(f"{tag}_rstd"), 2)
            for t in range(NT):
                nc.vector.tensor_scalar(dst[:, t, :], src[:, t, :], mv[:, t, 0:1], rstd[:, t:t + 1],
                                        ALU.subtract, ALU.mult).then_inc(S(f"{tag}_normed"), 1)

        def norm_gpsimd(g, tag):
            g.wait_ge(S(f"{tag}_moments"), NT)
            nc.gpsimd.tensor_scalar(rstd[:, :], mv[:, :, 1], EPS, None, ALU.add).then_inc(S(f"{tag}_rstd"), 1)
            g.wait_ge(S(f"{tag}_rstd"), 1)
            nc.gpsimd.tensor_tensor(rstd[:, :], rstd[:, :], mhalf[:, :], ALU.pow).then_inc(S(f"{tag}_rstd"), 1)

        def turn_tensor(pe, tag, src, ready):
            for q in range(NQ):
                pe.wait_ge(ready, 4 * q + 4)
                for j in range(4):
                    last = nc.tensor.transpose(ps[:, q, j * P:(j + 1) * P], src[:, 4 * q + j, :], ident[:, :])
                last.then_inc(S(f"{tag}_turned"), 1)

        def turn_scalar(act, tag, dst, gain=None, shift=None):
            for q in (0, 2):
                act.wait_ge(S(f"{tag}_turned"), q + 1)
                d = dst[:, q * QW:(q + 1) * QW]
                if gain is None:
                    nc.scalar.activation(d, ps[:, q, :], ACT.Copy).then_inc(S(f"{tag}_even"), 1)
                else:
                    nc.scalar.activation(d, ps[:, q, :], ACT.Identity, bias=shift, scale=gain).then_inc(S(f"{tag}_even"), 1)

        def turn_vector(ve, tag, dst, gain=None, shift=None):
            for q in (1, 3):
                ve.wait_ge(S(f"{tag}_turned"), q + 1)
                d = dst[:, q * QW:(q + 1) * QW]
                if gain is None:
                    nc.vector.tensor_copy(d, ps[:, q, :]).then_inc(S(f"{tag}_odd"), 1)
                else:
                    nc.vector.tensor_scalar(d, ps[:, q, :], gain, shift, ALU.mult, ALU.add).then_inc(S(f"{tag}_odd"), 1)

        def turned_wait(eng, tag, q):
            eng.wait_ge(S(f"{tag}_odd" if q % 2 else f"{tag}_even"), q // 2 + 1)

        def split_vector(ve, tag, src, b):
            c = slice(b * N, (b + 1) * N)
            done = S(f"{tag}_split")
            res = HN[:, :, :].rearrange("p t c -> p (t c)")
            nc.vector.tensor_copy(parts[:, 0, c], src[:, c]).then_inc(done, 1)
            ve.wait_ge(done, 4 * b + 1)
            nc.vector.tensor_tensor(res[:, c], src[:, c], parts[:, 0, c], ALU.subtract).then_inc(done, 1)
            ve.wait_ge(done, 4 * b + 2)
            nc.vector.tensor_copy(parts[:, 1, c], res[:, c]).then_inc(done, 1)
            ve.wait_ge(done, 4 * b + 3)
            nc.vector.tensor_tensor(parts[:, 2, c], res[:, c], parts[:, 1, c], ALU.subtract).then_inc(done, 1)

        def stack_sync(sp, tag, dst, order, b, at):
            sp.wait_ge(S(f"{tag}_split"), 4 * b + 4)
            for r, part in enumerate(order):
                sp.dma_start(dst.rearrange("h (r d) t -> r h d t", r=NR)[r, :, :, at:at + N],
                             parts[:, part, b * N:(b + 1) * N]).then_inc(S(f"{tag}_stacked"), 16)

        def qk_tensor(pe, tag, w, turned):
            for q in range(NQ):
                turned_wait(pe, turned, q)
                for which in range(2):
                    nc.tensor.matmul(ps[:, 4 * which + q, :], w[:, which * P:(which + 1) * P],
                                     XT[:, q * QW:(q + 1) * QW], start=True, stop=True).then_inc(S(f"{tag}_qk"), 1)

        def v_tensor(pe, tag, w):
            for q in range(NQ):
                pe.wait_ge(S(f"{tag}_q_out"), q + 1)
                for j in range(4):
                    t = 4 * q + j
                    last = nc.tensor.matmul(ps[:, q, j * P:(j + 1) * P], XT[:, t * P:(t + 1) * P], w[:, 2 * P:3 * P],
                                            start=True, stop=True)
                last.then_inc(S(f"{tag}_v"), 1)

        def route_tensor(pe, m):
            for q in range(NQ):
                turned_wait(pe, m, q)
            for t in range(NT):
                last = nc.tensor.matmul(ps[:, 4, t * E:(t + 1) * E], XT[:, t * P:(t + 1) * P], rw[:, :],
                                        start=True, stop=True)
            last.then_inc(S(f"{m}_logits"), 1)

        def route_vector(ve, m):
            done = S(f"{m}_route")
            n = [0]

            def step(ins):
                n[0] += 1
                ins.then_inc(done, 1)
                ve.wait_ge(done, n[0])

            ve.wait_ge(S(f"{m}_logits"), 1)
            step(nc.vector.tensor_copy(L[:, :, :].rearrange("p t e -> p (t e)"), ps[:, 4, 0:NT * E]))
            mine = L[:, :, :].unsqueeze(3).broadcast_to([P, NT, E, E])
            theirs = L[:, :, :].unsqueeze(2).broadcast_to([P, NT, E, E])
            step(nc.vector.tensor_tensor(ties[:, :, :, :], theirs, mine, ALU.is_equal))
            step(nc.vector.tensor_tensor(ties[:, :, :, :], ties[:, :, :, :],
                                         tri[:, :, :].unsqueeze(1).broadcast_to([P, NT, E, E]), ALU.mult))
            step(nc.vector.tensor_tensor(beats[:, :, :, :], theirs, mine, ALU.is_gt))
            step(nc.vector.tensor_tensor(beats[:, :, :, :], beats[:, :, :, :], ties[:, :, :, :], ALU.add))
            step(nc.vector.tensor_reduce(rank[:, :, :], beats[:, :, :, :], AX, ALU.add))
            step(nc.vector.tensor_reduce(lmax[:, :], L[:, :, :], AX, ALU.max))
            step(nc.vector.tensor_tensor(L[:, :, :], L[:, :, :], lmax[:, :].unsqueeze(2).broadcast_to([P, NT, E]),
                                         ALU.subtract))
            ve.wait_ge(S(f"{m}_exps"), 1)
            step(nc.vector.tensor_scalar(rank[:, :, :], rank[:, :, :], 2.0, None, ALU.is_lt))
            step(nc.vector.tensor_tensor(comb[:, :, :], comb[:, :, :], rank[:, :, :], ALU.mult))
            step(nc.vector.tensor_reduce(lmax[:, :], comb[:, :, :], AX, ALU.add))
            step(nc.vector.reciprocal(lmax[:, :], lmax[:, :]))
            nc.vector.tensor_tensor(comb[:, :, :], comb[:, :, :], lmax[:, :].unsqueeze(2).broadcast_to([P, NT, E]),
                                    ALU.mult).then_inc(S(f"{m}_comb"), 1)

        def route_scalar(act, m):
            act.wait_ge(S(f"{m}_route"), 8)
            nc.scalar.activation(comb[:, :, :], L[:, :, :], ACT.Exp).then_inc(S(f"{m}_exps"), 1)

        def bias2_tensor(pe, m):
            pe.wait_ge(S(f"{m}_comb"), 1)
            for t in range(NT):
                last = nc.tensor.transpose(ps[0:E, 4 + t // 4, (t % 4) * P:(t % 4 + 1) * P], comb[:, t, :], ident[:, :])
            last.then_inc(S(f"{m}_combT"), 1)
            pe.wait_ge(S(f"{m}_combT_out"), 1)
            for t in range(NT):
                last = nc.tensor.matmul(ps[:, 4 + t // 4, (t % 4) * P:(t % 4 + 1) * P], combT[:, t * P:(t + 1) * P],
                                        b2e[:, :], start=True, stop=True)
            last.then_inc(S(f"{m}_bias2"), 1)

        def bias2_vector(ve, m):
            ve.wait_ge(S(f"{m}_combT"), 1)
            nc.vector.tensor_copy(combT, ps[0:E, 4:8, :].rearrange("p a n -> p (a n)")).then_inc(S(f"{m}_combT_out"), 1)
            ve.wait_ge(S(f"{m}_bias2"), 1)
            xf = X[:, :, :].rearrange("p t c -> p (t c)")
            nc.vector.tensor_tensor(xf, xf, ps[:, 4:8, :].rearrange("p a n -> p (a n)"), ALU.add)\
              .then_inc(S(f"{m}_bias2_in"), 1)

        def expert_up(i, s):
            for f in range(FC):
                nc.tensor.wait_ge(S("gelu_out"), 32 * i + 4 * s + f + 1)
                nc.tensor.matmul(ps[:, f, :], W1s[s // 4][:, f * P:(f + 1) * P],
                                 XT[:, (s % 4) * QW:(s % 4 + 1) * QW], start=True, stop=True).then_inc(S("up_done"), 1)

        def expert_down(i, s):
            nc.tensor.wait_ge(S("gelu_out"), 32 * i + 4 * s + 8)
            nc.tensor.wait_ge(S("y_used"), 8 * i + s + 1)
            for j in range(4):
                for f in range(FC):
                    last = nc.tensor.matmul(ps[:, 4 + s % 2, j * P:(j + 1) * P], PE_[s % 2][:, f, j * P:(j + 1) * P],
                                            W2s[s // 4][:, f, :], start=(f == 0), stop=(f == FC - 1))
            last.then_inc(S("down_done"), 1)

        def experts_tensor(pe, m, r):
            pe.wait_ge(S(f"{m}_bias2_in"), 1)
            with pe.Fori(4 * r, 4 * r + 4) as i:
                for s in range(8):
                    if s % 4 == 0:
                        pe.wait_ge(S(f"w_in{s // 4}"), 32 * i + 32)
                    expert_up(i, s)
                    if s:
                        expert_down(i, s - 1)
                expert_down(i, 7)

        def experts_scalar(act, m, r):
            with act.Fori(4 * r, 4 * r + 4) as i:
                for s in range(8):
                    if s % 4 == 0:
                        act.wait_ge(S("b1_in"), 2 * i + s // 4 + 1)
                    for f in range(FC):
                        act.wait_ge(S("up_done"), 32 * i + 4 * s + f + 1)
                        if f == 0:
                            act.wait_ge(S("down_done"), 8 * i + s + 1)
                        nc.scalar.activation(PE_[s % 2][:, f, :], ps[:, f, :], ACT.Gelu,
                                             bias=b1s[:, s // 4, f:f + 1]).then_inc(S("gelu_out"), 1)

        def experts_vector(ve, m, r):
            with ve.Fori(4 * r, 4 * r + 4) as i:
                for s in range(8):
                    if s % 4 == 0:
                        ve.wait_ge(S("cw_in"), 2 * i + s // 4 + 1)
                    ve.wait_ge(S("down_done"), 8 * i + s + 3)
                    for j in range(4):
                        t = 4 * (s % 4) + j
                        last = nc.vector.scalar_tensor_tensor(X[:, t, :], ps[:, 4 + s % 2, j * P:(j + 1) * P],
                                                              cw[:, s // 4, t:t + 1], X[:, t, :], ALU.mult, ALU.add)
                    last.then_inc(S("y_used"), 1)

        def experts_gpsimd(g, m, r):
            g.wait_ge(S(f"{m}_comb"), 1)
            with g.Fori(4 * r, 4 * r + 4) as i:
                for p in range(2):
                    hold(g, S("y_used"), 8 * i + (2 if p else 1))
                    e = 2 * (i - 4 * r) + p
                    nc.gpsimd.tensor_copy(cw[:, p, :].unsqueeze(2), comb[:, :, bass.ds(e, 1)]).then_inc(S("cw_in"), 1)
                    nc.gpsimd.tensor_copy(b1s[:, p, :].unsqueeze(1), b1e[:, bass.ds(e, 1), :]).then_inc(S("b1_in"), 1)

        def experts_sync(sp, m, r):
            sp.wait_ge(S(f"{m}_logits"), 1)
            with sp.Fori(4 * r, 4 * r + 4) as i:
                for p in range(2):
                    hold(sp, S("down_done"), 8 * i + (2 if p else 1))
                    e = 2 * (i - 4 * r) + p
                    sp.dma_start(W1s[p], dram["ffn_w1"][bass.ds(e, 1), :, :].rearrange("e p f -> p (e f)"))\
                      .then_inc(S(f"w_in{p}"), 16)
                    sp.dma_start(W2s[p], dram["ffn_w2"][bass.ds(e, 1), :, :, :].rearrange("e p f c -> p (e f) c"))\
                      .then_inc(S(f"w_in{p}"), 16)

        @block.sync
        def _(sp):
            for name, dst in (("wqkva", wqkva), ("ident", ident), ("wpa", wpa), ("bpa", bpa), ("sel", sel),
                              ("wqkvb", wqkvb), ("colb", colb), ("bvb", bvb), ("bob", bob), ("b2b", b2b),
                              ("wob", wob), ("w1b", w1b), ("w2b", w2b), ("rw", rw), ("b1e", b1e), ("b2e", b2e),
                              ("tri", tri), ("causal", causal), ("identb", identb)):
                ap = dst[tuple(slice(None) for _ in dst.shape)]
                sp.dma_start(ap, dram[name]).then_inc(S("consts_in"), 16)
            for b in range(B):
                stack_sync(sp, "aq", qst, Q_PARTS, b, b * N)
            for b in range(B):
                stack_sync(sp, "ak", kst, K_PARTS, b, b * N)
            sp.wait_ge(S("aq_stacked"), 16 * NR * B)
            sp.wait_ge(S("ak_stacked"), 16 * NR * B)
            sp.wait_ge(S("qz_clear"), 4)

            def load(i, b):
                for j in range(2):
                    sp.dma_start(KA[b][KR * j:KR * j + KR, :, :], kst_q[i, j, :, :, b * N:(b + 1) * N])\
                      .then_inc(S(f"kq_in{b}"), 16)
                    sp.dma_start(QZ[b][KR * j:KR * j + KR, :, j, :], qst_q[i, j, :, :, b * N:(b + 1) * N])\
                      .then_inc(S(f"kq_in{b}"), 16)

            load(0, 0)
            load(0, 1)
            with sp.Fori(0, QUADS - 1) as i:
                for b in range(B):
                    hold(sp, S("exp_done"), 128 * i + 64 * b + 128)
                    load(i + 1, b)
            experts_sync(sp, "m0", 0)
            sp.wait_ge(S("zero_ready"), 3)
            for b in range(B):
                sp.dma_start(kstb[:, :, b * PADN:b * PADN + BK].rearrange("h r t -> (h r) t")
                             .rearrange("(p g) t -> p g t", g=H * KR // P),
                             zer[:, 0:BK].unsqueeze(1).broadcast_to([P, H * KR // 128, BK])).then_inc(S("bk_stacked"), 16)
                sp.dma_start(vst[b, 0:BK, :], zerf[:, :]).then_inc(S("bv_stored"), 16)
            for b in range(B):
                stack_sync(sp, "bq", qstb, Q_PARTS, b, b * N)
            for b in range(B):
                stack_sync(sp, "bk", kstb, K_PARTS, b, b * PADN + BK)
            sp.wait_ge(S("b_v_out"), NQ)
            for b in range(B):
                sp.dma_start(vst[b, BK:PADN, :].rearrange("(t p) c -> p t c", p=P),
                             V9[:, b * MT:(b + 1) * MT, :, :].rearrange("p t h c -> p t (h c)")).then_inc(S("bv_stored"), 16)
            sp.wait_ge(S("bq_stacked"), 16 * NR * B)
            sp.wait_ge(S("bk_stacked"), 16 * (NR * B + B))
            sp.wait_ge(S("bv_stored"), 16 * 2 * B)
            for b in range(B):
                with sp.Fori(b * MT // 2, (b + 1) * MT // 2) as i:
                    for j in range(2):
                        at = 2 * P * i + j * P
                        pad = at + BK * b
                        hold(sp, S("b_tile"), 2 * i + j + 1)
                        sp.dma_start(QB[j][0:KR, :, :], qstb[:, :, bass.ds(at, P)].rearrange("h r t -> r h t"))\
                          .then_inc(S(f"b_in{j}"), 16)
                        sp.dma_start(KB[j][0:KR, :, :], kstb[:, :, bass.ds(pad, P)].rearrange("h r t -> r h t"))\
                          .then_inc(S(f"b_in{j}"), 16)
                        sp.dma_start(KBx[j][0:KR, :, :], kstb[:, :, bass.ds(pad + P, BK)].rearrange("h r t -> r h t"))\
                          .then_inc(S(f"b_in{j}"), 16)
                        for w in range(2):
                            sp.dma_start(VWs[j][:, w, :], vst.rearrange("b n c -> (b n) c")[bass.ds(pad + BK * w, P), :])\
                              .then_inc(S(f"b_in{j}"), 16)
            experts_sync(sp, "m1", 1)
            sp.wait_ge(S("y_used"), 2 + 64)
            sp.dma_start(out.rearrange("b (t p) c -> p (b t) c", p=P), X[:, :, :]).then_inc(S("stored"), 16)
            sp.wait_ge(S("stored"), 16)

        @block.gpsimd
        def _(g):
            nc.gpsimd.memset(mhalf[:, :], -0.5).then_inc(S("half_ready"), 1)
            g.wait_ge(S("half_ready"), 1)
            norm_gpsimd(g, "na")
            for b in range(B):
                nc.gpsimd.memset(QZ[b][:, :, :, :], 0.0).then_inc(S("qz_clear"), 1)
                nc.gpsimd.memset(KA[b][:, :, :], 1.0).then_inc(S("qz_clear"), 1)
                nc.gpsimd.memset(Vs[b][:, :, :, :], 0.0).then_inc(S("vs_set"), 1)
                g.wait_ge(S("vs_set"), 2 * b + 1)
                nc.gpsimd.memset(Vs[b][:, :, :, D:D + 1], 1.0).then_inc(S("vs_set"), 1)
            g.wait_ge(S("na_normed"), NT)
            g.wait_ge(S("consts_in"), 16 * 19)
            nc.gpsimd.tensor_tensor(X[:, :, :], X[:, :, :], bpa[:, :].unsqueeze(1).broadcast_to([P, NT, P]),
                                    ALU.add).then_inc(S("x_biased"), 1)
            g.wait_ge(S("vs_set"), 4)
            g.wait_ge(S("a_v_out"), NQ)

            def values(i, b):
                nc.gpsimd.tensor_copy(Vs[b][:, :, :, 0:D],
                                      Vn[:, bass.ds(B * i + b, 1), :, :].rearrange("p o m (h d) -> p (o m) h d", h=HQ))\
                  .then_inc(S("vs_in"), 1)

            def max_rows(i, b, nh):
                c = B * i + b
                hold(g, S("max_done"), ITEMS * c + TURN_AT[nh] + 1)
                if not (isinstance(c, int) and c == 0):
                    hold(g, S(f"mrow_out{nh}"), 16 * c)
                q = S("msplit")
                k = 8 * c + 4 * nh
                nc.gpsimd.tensor_copy(mparts[nh][:, 0, :], neg[nh][:, :]).then_inc(q, 1)
                hold(g, q, k + 1)
                nc.gpsimd.tensor_tensor(nres[:, :], neg[nh][:, :], mparts[nh][:, 0, :], ALU.subtract).then_inc(q, 1)
                hold(g, q, k + 2)
                nc.gpsimd.tensor_copy(mparts[nh][:, 1, :], nres[:, :]).then_inc(q, 1)
                hold(g, q, k + 3)
                nc.gpsimd.tensor_tensor(mparts[nh][:, 2, :], nres[:, :], mparts[nh][:, 1, :], ALU.subtract).then_inc(q, 1)
                hold(g, q, k + 4)
                g.dma_start(mrow[b, nh].rearrange("s c n -> c s n"), mparts[nh][:, :, :]).then_inc(S(f"mrow_out{nh}"), 16)
                hold(g, S(f"mrow_out{nh}"), 16 * c + 16)
                g.dma_start(QZ[b][96:99, :, :, nh * 512:(nh + 1) * 512].rearrange("s a j n -> s (a j) n"),
                            mrow[b, nh].rearrange("s (h t) n -> s h (t n)", h=HQ)).then_inc(S(f"mrow_in{b}{nh}"), 16)

            for nh in range(2):
                max_rows(0, 0, nh)
            values(0, 0)
            values(0, 1)

            def follow(i, b, last):
                if not (last and b == 1):
                    for nh in range(2):
                        max_rows(i + b, 1 - b, nh)
                if not last:
                    hold(g, S("pv_done"), 2 + 32 * i + 16 * b + 16)
                    values(i + 1, b)

            with g.Fori(0, QUADS - 1) as i:
                for b in range(B):
                    follow(i, b, False)
            for b in range(B):
                follow(QUADS - 1, b, True)
            for k in range(QUADS * NQ):
                g.wait_ge(S("rden_ready"), k + 1)
                o = OT[:, k // NQ, (k % NQ) * QW:(k % NQ + 1) * QW]
                nc.gpsimd.tensor_tensor(o, o, rden[:, k % 2, :], ALU.mult).then_inc(S("o_normed"), 1)

            norm_gpsimd(g, "n0")
            experts_gpsimd(g, "m0", 0)
            norm_gpsimd(g, "nb")
            norm_gpsimd(g, "nb1")
            nc.gpsimd.memset(zer[:, :], 0.0).then_inc(S("zero_ready"), 1)
            nc.gpsimd.memset(zerf[:, :], 0.0).then_inc(S("zero_ready"), 1)
            g.wait_ge(S("zero_ready"), 2)
            nc.gpsimd.memset(zerf[:, :].rearrange("p (h c) -> p h c", c=VW)[:, :, D:], 1.0).then_inc(S("zero_ready"), 1)
            nc.gpsimd.memset(V9[:, :, :, D:D + 1], 1.0).then_inc(S("v9_ones"), 1)
            g.wait_ge(S("nb1_normed"), NT)
            nc.gpsimd.tensor_tensor(XN[:, :, :], XN[:, :, :], bob[:, :].unsqueeze(1).broadcast_to([P, NT, P]),
                                    ALU.add).then_inc(S("xn_biased"), 1)
            norm_gpsimd(g, "nb2")
            g.wait_ge(S("nb2_normed"), NT)
            nc.gpsimd.tensor_tensor(XN[:, :, :], XN[:, :, :], b2b[:, :].unsqueeze(1).broadcast_to([P, NT, P]),
                                    ALU.add).then_inc(S("xn_biased"), 1)
            g.wait_ge(S("xn_biased"), 2)
            nc.gpsimd.tensor_tensor(X[:, :, :], X[:, :, :], XN[:, :, :], ALU.add).then_inc(S("x_plus"), 1)
            norm_gpsimd(g, "n1")
            experts_gpsimd(g, "m1", 1)

        @block.scalar
        def _(act):
            act.dma_start(X[:, :, :], dram["x"].rearrange("b (t p) c -> p (b t) c", p=P)).then_inc(S("x_in"), 16)
            act.nop().then_inc(S("exp_done"), 64)
            turn_scalar(act, "na", XT)

            for q in range(NQ):
                act.wait_ge(S("a_qk"), 2 * q + 1)
                nc.scalar.activation(QF[:, q * QW:(q + 1) * QW], ps[:, q, :], ACT.Copy, scale=SCALE).then_inc(S("a_q_out"), 1)
                act.wait_ge(S("a_qk"), 2 * q + 2)
                nc.scalar.activation(KF[:, q * QW:(q + 1) * QW], ps[:, 4 + q, :], ACT.Copy).then_inc(S("a_k_out"), 1)
            for q in range(NQ):
                act.wait_ge(S("a_v"), q + 1)
                b, m = q // 2, q % 2
                for quad in range(QUADS):
                    ins = nc.scalar.activation(
                        Vn[:, B * quad + b, 4 * m:4 * m + 4, :],
                        ps[:, q, :].rearrange("p (m c) -> p m c", m=4)[:, :, 32 * quad:32 * quad + 32], ACT.Copy)
                ins.then_inc(S("a_v_out"), 1)

            def unit(i, b, u):
                for h in range(HQ):
                    k = 4 * u + h
                    act.wait_ge(S("s_full"), 128 * i + 64 * b + k + 1)
                    if h == 0:
                        act.wait_ge(S("pv_done"), 32 * i + 16 * b + u + 1)
                    nc.scalar.activation(PE_[u % 2][:, h, :], ps[:, SB[k % 3], :], ACT.Exp).then_inc(S("exp_done"), 1)

            def output(i, b, nh):
                act.wait_ge(S("pv_done"), 2 + 32 * i + 16 * b + 8 * nh + 8)
                nc.scalar.activation(OT[:, bass.ds(i, 1), b * N + nh * 512:b * N + (nh + 1) * 512],
                                     ps[:, OB, :].unsqueeze(1), ACT.Copy).then_inc(S("o_out"), 1)

            with act.Fori(0, QUADS) as i:
                for b in range(B):
                    for u in range(UNITS):
                        unit(i, b, u)
                        if u == MT:
                            output(i, b, 0)
                    output(i, b, 1)

            turn_scalar(act, "m0", XT)
            route_scalar(act, "m0")
            act.nop().then_inc(S("gelu_out"), 4)
            experts_scalar(act, "m0", 0)
            turn_scalar(act, "b1", XT, colb[:, LN1G:LN1G + 1], colb[:, LN1B:LN1B + 1])
            for q in range(NQ):
                act.wait_ge(S("b_qk"), 2 * q + 2)
                nc.scalar.activation(KF[:, q * QW:(q + 1) * QW], ps[:, 4 + q, :], ACT.Identity,
                                     bias=colb[:, BKC:BKC + 1]).then_inc(S("b_k_out"), 1)
            with act.Fori(0, NT // 2) as i:
                for j in range(2):
                    act.wait_ge(S("b_shifted"), 2 * i + j + 1)
                    nc.scalar.activation(PB, PB, ACT.Exp).then_inc(S("b_exp"), 1)
                    act.wait_ge(S("b_pturned"), 4 * i + 2 * j + 1)
                    nc.scalar.activation(PT[:, 0:8, :], ps[:, 4:6, :].rearrange("p a (h n) -> p (a h) n", h=4),
                                         ACT.Copy).then_inc(S("b_pt_even"), 1)
            turn_scalar(act, "bo", XT)
            turn_scalar(act, "b2", XT, colb[:, LN2G:LN2G + 1], colb[:, LN2B:LN2B + 1])
            for s in range(NQ):
                for f in range(FC):
                    act.wait_ge(S("mlp_up"), 4 * s + f + 1)
                    if f == 0 and s >= 2:
                        act.wait_ge(S("mlp_down"), s - 1)
                    nc.scalar.activation(PE_[s % 2][:, f, :], ps[:, f, :], ACT.Gelu,
                                         bias=colb[:, B1C + f:B1C + f + 1]).then_inc(S("mlp_gelu"), 1)
            turn_scalar(act, "m1", XT)
            route_scalar(act, "m1")
            experts_scalar(act, "m1", 1)

        @block.vector
        def _(ve):
            ve.nop().then_inc(S("y_used"), 2)
            ve.wait_ge(S("x_in"), 16)
            norm_vector(ve, "na", X, XN)
            turn_vector(ve, "na", XT)
            for b in range(B):
                ve.wait_ge(S("a_q_out"), 2 * b + 2)
                split_vector(ve, "aq", QF, b)
            ve.wait_ge(S("aq_stacked"), 16 * NR * B)
            for b in range(B):
                ve.wait_ge(S("a_k_out"), 2 * b + 2)
                split_vector(ve, "ak", KF, b)

            def maxima(i, b):
                c = B * i + b
                for k, item in enumerate(ITEM_LIST):
                    ve.wait_ge(S("max_full"), ITEMS * c + k + 1)
                    nh = item[1]
                    if item[0] == "max":
                        _, _, h, nt = item
                        nc.vector.tensor_reduce(mx[nh][:, 4 * h + nt:4 * h + nt + 1],
                                                ps[:, MB[k % 2]:MB[k % 2] + 2, :].rearrange("p a n -> p (a n)"), AX, ALU.max)\
                          .then_inc(S("max_done"), 1)
                    else:
                        if not (isinstance(c, int) and c == 0):
                            ve.wait_ge(S("msplit"), 8 * c - 8 + 4 * nh + 4)
                        nc.vector.tensor_scalar(neg[nh][:, :], ps[0:16, MB[k % 2], 0:P], -1.0, None, ALU.mult)\
                          .then_inc(S("max_done"), 1)

            maxima(0, 0)
            with ve.Fori(0, QUADS - 1) as i:
                maxima(i, 1)
                maxima(i + 1, 0)
            maxima(QUADS - 1, 1)
            for k in range(QUADS * NQ):
                ve.wait_ge(S("den_full"), k + 1)
                if k >= 2:
                    ve.wait_ge(S("o_normed"), k - 1)
                nc.vector.reciprocal(rden[:, k % 2, :], ps[:, k % 2, :]).then_inc(S("rden_ready"), 1)
            ve.wait_ge(S("x_biased"), 1)
            for q in range(NQ):
                ve.wait_ge(S("a_proj"), q + 1)
                xq = X[:, 4 * q:4 * q + 4, :].rearrange("p t c -> p (t c)")
                nc.vector.tensor_tensor(xq, xq, ps[:, 4 + q, :], ALU.add).then_inc(S("x1"), 1)
            ve.wait_ge(S("x1"), NQ)
            norm_vector(ve, "n0", X, XN)
            turn_vector(ve, "m0", XT)
            route_vector(ve, "m0")
            bias2_vector(ve, "m0")
            ve.wait_ge(S("m0_bias2_in"), 1)
            experts_vector(ve, "m0", 0)
            ve.wait_ge(S("y_used"), 2 + 32)
            norm_vector(ve, "nb", X, XN)
            ve.wait_ge(S("nb_normed"), NT)
            norm_vector(ve, "nb1", XN, HN)
            turn_vector(ve, "b1", XT, colb[:, LN1G:LN1G + 1], colb[:, LN1B:LN1B + 1])
            for q in range(NQ):
                ve.wait_ge(S("b_qk"), 2 * q + 1)
                nc.vector.tensor_scalar(QF[:, q * QW:(q + 1) * QW], ps[:, q, :], colb[:, BQ:BQ + 1], SCALE,
                                        ALU.add, ALU.mult).then_inc(S("b_q_out"), 1)
            ve.wait_ge(S("v9_ones"), 1)
            for q in range(NQ):
                ve.wait_ge(S("b_v"), q + 1)
                for j in range(4):
                    t = 4 * q + j
                    ins = nc.vector.tensor_tensor(V9[:, t, :, 0:D],
                                                  ps[:, q, j * P:(j + 1) * P].rearrange("p (h d) -> p h d", h=H),
                                                  bvb[:, :].rearrange("p (h d) -> p h d", h=H), ALU.add)
                ins.then_inc(S("b_v_out"), 1)
            ve.wait_ge(S("b_q_out"), NQ)
            for b in range(B):
                split_vector(ve, "bq", QF, b)
            ve.wait_ge(S("bq_stacked"), 16 * NR * B)
            for b in range(B):
                ve.wait_ge(S("b_k_out"), 2 * b + 2)
                split_vector(ve, "bk", KF, b)
            with ve.Fori(0, NT // 2) as i:
                for j in range(2):
                    t = 2 * i + j
                    ve.wait_ge(S("b_scores"), t + 1)
                    sc = ps[:, 0:4, :].rearrange("p a (h n) -> p (a h) n", h=4)
                    nc.vector.tensor_reduce(mxb[:, :], sc, AX, ALU.max).then_inc(S("b_max"), 1)
                    ve.wait_ge(S("b_max"), t + 1)
                    ve.wait_ge(S("b_pt_free"), t + 1)
                    nc.vector.tensor_tensor(PB, sc, mxb[:, :].unsqueeze(2).broadcast_to([P, H, P]), ALU.subtract)\
                      .then_inc(S("b_shifted"), 1)
                    ve.wait_ge(S("b_pturned"), 4 * i + 2 * j + 2)
                    nc.vector.tensor_copy(PT[:, 8:16, :], ps[:, 6:8, :].rearrange("p a (h n) -> p (a h) n", h=4))\
                      .then_inc(S("b_pt_odd"), 1)
                    ve.wait_ge(S("b_pv"), t + 1)
                    o = ps[:, 4, 0:H * VW].rearrange("p (h c) -> p h c", h=H)
                    nc.vector.reciprocal(rsb[:, :], o[:, :, D]).then_inc(S("b_rs"), 1)
                    ve.wait_ge(S("b_rs"), t + 1)
                    nc.vector.tensor_tensor(AO[:, bass.ds(t, 1), :, :].rearrange("p t h d -> p (t h) d"), o[:, :, 0:D],
                                            rsb[:, :].unsqueeze(2).broadcast_to([P, H, D]), ALU.mult)\
                      .then_inc(S("b_tile"), 1)
            turn_vector(ve, "bo", XT)
            ve.wait_ge(S("xn_biased"), 1)
            for q in range(NQ):
                ve.wait_ge(S("b_proj"), q + 1)
                xq = XN[:, 4 * q:4 * q + 4, :].rearrange("p t c -> p (t c)")
                nc.vector.tensor_tensor(xq, xq, ps[:, 4 + q, :], ALU.add).then_inc(S("xb1"), 1)
            ve.wait_ge(S("xb1"), NQ)
            norm_vector(ve, "nb2", XN, HN)
            turn_vector(ve, "b2", XT, colb[:, LN2G:LN2G + 1], colb[:, LN2B:LN2B + 1])
            ve.wait_ge(S("x_plus"), 1)
            for s in range(NQ):
                ve.wait_ge(S("mlp_down"), s + 1)
                xq = X[:, 4 * s:4 * s + 4, :].rearrange("p t c -> p (t c)")
                nc.vector.tensor_tensor(xq, xq, ps[:, 4 + s % 2, :], ALU.add).then_inc(S("x3"), 1)
            ve.wait_ge(S("x3"), NQ)
            norm_vector(ve, "n1", X, XN)
            turn_vector(ve, "m1", XT)
            route_vector(ve, "m1")
            bias2_vector(ve, "m1")
            ve.wait_ge(S("m1_bias2_in"), 1)
            experts_vector(ve, "m1", 1)

        @block.tensor
        def _(pe):
            pe.nop().then_inc(S("pv_done"), 2)
            pe.nop().then_inc(S("down_done"), 2)
            pe.wait_ge(S("consts_in"), 16 * 19)
            turn_tensor(pe, "na", XN, S("na_normed"))
            qk_tensor(pe, "a", wqkva, "na")
            v_tensor(pe, "a", wqkva)

            def max_item(i, b, k):
                c = B * i + b
                item = ITEM_LIST[k]
                first = isinstance(c, int) and c == 0
                if not (first and k < 2):
                    pe.wait_ge(S("max_done"), ITEMS * c + k - 1)
                if item[0] == "max":
                    _, nh, h, nt = item
                    n0 = 512 * nh + P * nt
                    for mh in range(2):
                        last = nc.tensor.matmul(ps[:, MB[k % 2] + mh, :], QZ[b][0:96, h // 2, h % 2, n0:n0 + P],
                                                KA[b][0:96, h // 2, 512 * mh:512 * mh + 512], start=True, stop=True)
                    last.then_inc(S("max_full"), 1)
                else:
                    nh = item[1]
                    pe.wait_ge(S("max_done"), ITEMS * c + LAST_MAX[nh] + 1)
                    nc.tensor.transpose(ps[0:16, MB[k % 2], 0:P], mx[nh][:, :], ident[:, :]).then_inc(S("max_full"), 1)

            def weigh(i, b, u):
                nh, mt = u // MT, u % MT
                pe.wait_ge(S("exp_done"), 64 + 128 * i + 64 * b + 4 * u + 4)
                if mt == 0:
                    if u == 0:
                        pe.wait_ge(S("vs_in"), 2 * i + b + 1)
                    pe.wait_ge(S("o_out"), 4 * i + 2 * b + nh + 1)
                for h in range(HQ):
                    last = nc.tensor.matmul(ps[32 * h:32 * h + 32, OB, :], Vs[b][:, mt, h, :], PE_[u % 2][:, h, :],
                                            start=(mt == 0), stop=(mt == MT - 1))
                last.then_inc(S("pv_done"), 1)

            def combination(i, b, more):
                items = list(range(ITEMS)) if more else []
                for u in range(UNITS):
                    nh, mt = u // MT, u % MT
                    todo = [items.pop(0) for _ in range(PLAN[u])] if more else []
                    if mt == 0:
                        pe.wait_ge(S(f"mrow_in{b}{nh}"), 16 * i + 16)
                    for h in range(HQ):
                        k = 4 * u + h
                        back = 3 if k >= 3 else {0: 1, 1: 4, 2: 4}[k]
                        pe.wait_ge(S("exp_done"), 64 + 128 * i + 64 * b + k - back + 1)
                        nc.tensor.matmul(ps[:, SB[k % 3], :], KA[b][0:99, h // 2, mt * P:(mt + 1) * P],
                                         QZ[b][0:99, h // 2, h % 2, 512 * nh:512 * nh + 512],
                                         start=True, stop=True).then_inc(S("s_full"), 1)
                        if todo and h < 3:
                            j = todo.pop(0)
                            if u == 1 and b == 0:
                                pe.wait_ge(S("kq_in1"), 64 * i + 64)
                            if u == 1 and b == 1:
                                pe.wait_ge(S("kq_in0"), 64 * i + 128)
                            max_item(i + b, 1 - b, j)
                    if u:
                        weigh(i, b, u - 1)
                weigh(i, b, UNITS - 1)

            pe.nop().then_inc(S("o_out"), 1)
            pe.wait_ge(S("kq_in0"), 64)
            pe.wait_ge(S("a_v_out"), NQ)
            pe.wait_ge(S("a_k_out"), NQ)
            for k in range(ITEMS):
                max_item(0, 0, k)
            with pe.Fori(0, QUADS - 1) as i:
                combination(i, 0, True)
                combination(i, 1, True)
            combination(QUADS - 1, 0, True)
            combination(QUADS - 1, 1, False)

            for k in range(QUADS * NQ):
                quad, q = k // NQ, k % NQ
                if k == 0:
                    pe.wait_ge(S("o_out"), 1 + 4 * QUADS)
                if k >= 2:
                    pe.wait_ge(S("rden_ready"), k - 1)
                nc.tensor.matmul(ps[:, k % 2, :], sel[:, :], OT[:, quad, q * QW:(q + 1) * QW], start=True, stop=True)\
                  .then_inc(S("den_full"), 1)
            pe.wait_ge(S("o_normed"), QUADS * NQ)
            for q in range(NQ):
                for j in range(4):
                    t = 4 * q + j
                    for quad in range(QUADS):
                        last = nc.tensor.matmul(ps[:, 4 + q, j * P:(j + 1) * P], OT[:, quad, t * P:(t + 1) * P],
                                                wpa[:, quad, :], start=(quad == 0), stop=(quad == QUADS - 1))
                last.then_inc(S("a_proj"), 1)
            turn_tensor(pe, "m0", XN, S("n0_normed"))
            route_tensor(pe, "m0")
            bias2_tensor(pe, "m0")
            experts_tensor(pe, "m0", 0)
            turn_tensor(pe, "b1", HN, S("nb1_normed"))
            qk_tensor(pe, "b", wqkvb, "b1")
            v_tensor(pe, "b", wqkvb)
            pe.wait_ge(S("b_v_out"), NQ)
            pe.wait_ge(S("b_k_out"), NQ)
            pe.nop().then_inc(S("b_tile"), 2)
            pe.nop().then_inc(S("b_pt_free"), 1)
            with pe.Fori(0, NT // 2) as i:
                for j in range(2):
                    t = 2 * i + j
                    pe.wait_ge(S(f"b_in{j}"), 80 * i + 80)
                    pe.wait_ge(S("b_tile"), t + 2)
                    for bank in range(4):
                        nc.tensor.matmul(ps[:, bank, :].rearrange("p (h n) -> p h n", h=4), identb[:, :],
                                         causal[:, :].unsqueeze(1).broadcast_to([P, 4, P]), start=True, stop=True,
                                         skip_group_check=True)
                        for hh in range(4):
                            h = 4 * bank + hh
                            c0 = hh * P
                            nc.tensor.matmul(ps[0:BK, bank, c0:c0 + P], QB[j][0:KR, h, 0:BK], KB[j][0:KR, h, :],
                                             start=False, stop=True, skip_group_check=True)
                            nc.tensor.matmul(ps[BK:P, bank, c0:c0 + BK], QB[j][0:KR, h, BK:P], KB[j][0:KR, h, BK:P],
                                             start=False, stop=True, skip_group_check=True)
                            last = nc.tensor.matmul(ps[BK:P, bank, c0 + BK:c0 + P], QB[j][0:KR, h, BK:P], KBx[j][0:KR, h, :],
                                                    start=False, stop=True, skip_group_check=True)
                    last.then_inc(S("b_scores"), 1)
                    pe.wait_ge(S("b_exp"), t + 1)
                    for half in range(2):
                        for hh in range(8):
                            h = 8 * half + hh
                            last = nc.tensor.transpose(ps[:, 4 + h // 4, (h % 4) * P:(h % 4 + 1) * P], PB[:, h, :], ident[:, :])
                        last.then_inc(S("b_pturned"), 1)
                    pe.wait_ge(S("b_pt_even"), t + 1)
                    pe.wait_ge(S("b_pt_odd"), t + 1)
                    pe.nop().then_inc(S("b_pt_free"), 1)
                    for w in range(2):
                        for h in range(H):
                            last = nc.tensor.matmul(ps[BK * w:BK * w + BK, 4, VW * h:VW * h + VW],
                                                    PT[:, h, BK * w:BK * w + BK],
                                                    VWs[j][:, w, VW * h:VW * h + VW], start=True, stop=True,
                                                    skip_group_check=True)
                    last.then_inc(S("b_pv"), 1)
            pe.wait_ge(S("b_tile"), 2 + NT)
            turn_tensor(pe, "bo", AO.rearrange("p t h d -> p t (h d)"), S("b_tile"))
            for q in range(NQ):
                turned_wait(pe, "bo", q)
                for j in range(4):
                    t = 4 * q + j
                    last = nc.tensor.matmul(ps[:, 4 + q, j * P:(j + 1) * P], XT[:, t * P:(t + 1) * P], wob[:, :],
                                            start=True, stop=True)
                last.then_inc(S("b_proj"), 1)
            turn_tensor(pe, "b2", HN, S("nb2_normed"))
            for q in range(NQ):
                turned_wait(pe, "b2", q)

            def mlp_down(s):
                pe.wait_ge(S("mlp_gelu"), 4 * s + 4)
                if s >= 2:
                    pe.wait_ge(S("x3"), s - 1)
                else:
                    pe.wait_ge(S("xb1"), NQ)
                for j in range(4):
                    for f in range(FC):
                        last = nc.tensor.matmul(ps[:, 4 + s % 2, j * P:(j + 1) * P], PE_[s % 2][:, f, j * P:(j + 1) * P],
                                                w2b[:, f, :], start=(f == 0), stop=(f == FC - 1))
                last.then_inc(S("mlp_down"), 1)

            for s in range(NQ):
                for f in range(FC):
                    if s:
                        pe.wait_ge(S("mlp_gelu"), 4 * s - 3 + f)
                    nc.tensor.matmul(ps[:, f, :], w1b[:, f * P:(f + 1) * P], XT[:, s * QW:(s + 1) * QW],
                                     start=True, stop=True).then_inc(S("mlp_up"), 1)
                if s:
                    mlp_down(s - 1)
            mlp_down(NQ - 1)
            turn_tensor(pe, "m1", XN, S("n1_normed"))
            route_tensor(pe, "m1")
            bias2_tensor(pe, "m1")
            experts_tensor(pe, "m1", 1)


def kernel(**inputs):
    import numpy as np
    import concourse.bacc as bacc
    from concourse.bass_utils import run_bass_kernel_spmd

    a = {k: np.ascontiguousarray(v) for k, v in inputs.items()}
    import ml_dtypes
    f32 = np.float32

    def blockdiag(w):
        g, ci, co = w.shape
        full = np.zeros((g * ci, g * co), f32)
        for k in range(g):
            full[k * ci:(k + 1) * ci, k * co:(k + 1) * co] = w[k]
        return full

    def rows(v):
        return np.ascontiguousarray(np.broadcast_to(v, (P, v.shape[0])))

    wp = blockdiag(a["L0_attn_a_w_proj"])
    wpa = np.zeros((P, QUADS, P), f32)
    sel = np.zeros((P, P), f32)
    for j in range(HQ):
        for quad in range(QUADS):
            h = HQ * quad + j
            wpa[32 * j:32 * j + D, quad, :] = wp[h * D:(h + 1) * D, :]
        sel[32 * j + D, 32 * j:32 * j + 32] = 1.0
    bq = a["L0_attn_b_b_qkv"]
    cols = [a["L0_attn_b_ln1_g"], a["L0_attn_b_ln1_b"], a["L0_attn_b_ln2_g"], a["L0_attn_b_ln2_b"],
            bq[0:P], bq[P:2 * P]] + [a["L0_attn_b_b1"][f * P:(f + 1) * P] for f in range(FC)]
    cols += [np.zeros(P, f32)] * (12 - len(cols))
    causal = np.zeros((P, P), f32)
    for i in range(P):
        causal[i, BK + i % BK + 1:] = -1e30
    arrays = {
        "x": a["L0_attn_a_x"],
        "wqkva": blockdiag(a["L0_attn_a_w_qkv"]), "wpa": wpa, "bpa": rows(a["L0_attn_a_b_proj"]), "sel": sel,
        "ident": np.eye(P, dtype=f32), "identb": np.eye(P, dtype=ml_dtypes.bfloat16),
        "causal": causal.astype(ml_dtypes.bfloat16),
        "tri": np.ascontiguousarray(np.broadcast_to(np.tril(np.ones((E, E), f32), -1), (P, E, E))),
        "wqkvb": a["L0_attn_b_w_qkv"], "colb": np.ascontiguousarray(np.stack(cols, axis=1)),
        "bvb": rows(bq[2 * P:3 * P]), "bob": rows(a["L0_attn_b_b_out"]), "b2b": rows(a["L0_attn_b_b2"]),
        "wob": a["L0_attn_b_w_out"], "w1b": a["L0_attn_b_w1"],
        "w2b": np.ascontiguousarray(a["L0_attn_b_w2"].reshape(FC, P, P).transpose(1, 0, 2)),
        "rw": np.ascontiguousarray(a["L0_ffn_router_w"].T),
        "b1e": np.ascontiguousarray(a["L0_ffn_b1"].reshape(E, FC, P).transpose(2, 0, 1)),
        "b2e": a["L0_ffn_b2"],
        "ffn_w1": np.ascontiguousarray(a["L0_ffn_w1"].transpose(0, 2, 1)),
        "ffn_w2": np.ascontiguousarray(a["L0_ffn_w2"].reshape(E, P, FC, P).transpose(0, 3, 2, 1)),
    }
    nc = bacc.Bacc("TRN2", target_bir_lowering=False, num_devices=1)
    dram = {k: nc.dram_tensor(f"in_{k}", v.shape, mybir.dt.from_np(v.dtype), kind="ExternalInput").ap()
            for k, v in arrays.items()}
    out = nc.dram_tensor("out", (B, N, P), F32, kind="ExternalOutput").ap()
    build(nc, dram, out)
    r = run_bass_kernel_spmd(nc, [{f"in_{k}": v for k, v in arrays.items()}], core_ids=[0])
    return r.results[0]["out"]
```

```python
from contextlib import ExitStack

import concourse.bass as bass
from concourse import mybir

F32 = mybir.dt.float32
F32R = mybir.dt.float32r
BF16 = mybir.dt.bfloat16
ALU = mybir.AluOpType
ACT = mybir.ActivationFunctionType
AX = mybir.AxisListType.X

P = 128
B = 2
N = 1024
T = B * N
NT = T // P
NQ = 4
QW = T // NQ
H = 16
D = P // H
HQ = 4
QUADS = H // HQ
SCALE = float(D) ** -0.5
EPS = 1e-5
K_PARTS = (0, 0, 0, 1, 1, 2)
Q_PARTS = (0, 1, 2, 0, 1, 0)
NR = len(K_PARTS)
KR = NR * D
MT = N // P
UNITS = 2 * MT
ITEMS = 34
E = 8
FF = 512
FC = FF // P
BK = 64
KW = 3 * BK
HH = H // 2
BU = 2 * NT
PADN = N + BK
VW = D + 1
CARRY = 12
PLAN = (3, 2, 2, 3, 2, 0, 3, 3, 2, 3, 2, 2, 3, 1, 1, 2)
assert sum(PLAN[:6]) == CARRY and sum(PLAN[6:]) == ITEMS - CARRY


def max_items():
    halves = [[("max", nh, h, nt) for nt in range(4) for h in range(HQ)] for nh in range(2)]
    return halves[0] + halves[1][:1] + [("turn", 0)] + halves[1][1:] + [("turn", 1)]


ITEM_LIST = max_items()
assert len(ITEM_LIST) == ITEMS
LAST_MAX = {0: 15, 1: 32}
TURN_AT = {0: 17, 1: 33}


def build(nc, dram, out):
    with ExitStack() as ctx:
        def sb(name, shape, dt=F32):
            return ctx.enter_context(nc.sbuf_tensor(name, shape, dt))

        def scratch(name, shape, dt):
            return nc.dram_tensor(name, shape, dt, kind="Internal").ap()

        sems = {}

        def S(name):
            if name not in sems:
                sems[name] = ctx.enter_context(nc.semaphore(name))
            return sems[name]

        X = sb("X", [P, NT, P])
        XN = sb("XN", [P, NT, P])
        HN = sb("HN", [P, NT, P])
        XT = sb("XT", [P, T])
        st = sb("st", [P, NT, 6])
        mv = sb("mv", [P, NT, 2])
        rstd = sb("rstd", [P, NT])
        mhalf = sb("mhalf", [P, NT])
        ident = sb("ident", [P, P])
        identb = sb("identb", [P, P], BF16)
        causal = sb("causal", [P, P], BF16)
        wqkva = sb("wqkva", [P, 3 * P])
        wpa = sb("wpa", [P, P])
        rsa = sb("rsa", [P, NT, H])
        bpa = sb("bpa", [P, P])
        wqkvb = sb("wqkvb", [P, 3 * P])
        colb = sb("colb", [P, 12])
        bvb = sb("bvb", [P, P])
        bob = sb("bob", [P, P])
        b2b = sb("b2b", [P, P])
        wob = sb("wob", [P, P])
        w1b = sb("w1b", [P, FF])
        w2b = sb("w2b", [P, FC, P])
        rw = sb("rw", [P, E])
        b1e = sb("b1e", [P, E, FC])
        b1s = sb("b1s", [P, 2, FC])
        b2e = sb("b2e", [E, P])
        tri = sb("tri", [P, E, E], BF16)
        L = sb("L", [P, NT, E])
        beats = sb("beats", [P, NT, E, E], BF16)
        ties = sb("ties", [P, NT, E, E], BF16)
        rank = sb("rank", [P, NT, E])
        lmax = sb("lmax", [P, NT])
        comb = sb("comb", [P, NT, E])
        zer = sb("zer", [P, BK], BF16)

        with ExitStack() as phase:
            def pb(name, shape, dt=F32):
                return phase.enter_context(nc.sbuf_tensor(name, shape, dt))

            QF = pb("QF", [P, T])
            KF = pb("KF", [P, T])
            parts = pb("parts", [P, 3, T], BF16)
            KA = [pb(f"KA{b}", [P, 2, N], BF16) for b in range(B)]
            QZ = [pb(f"QZ{b}", [P, 2, 2, N], BF16) for b in range(B)]
            EX = [pb(f"EX{j}", [P, HQ, 512]) for j in range(2)]
            OT = pb("OT", [P, QUADS, T])
            Vn = pb("Vn", [P, QUADS * B, MT, HQ * D])
            Vs = [pb(f"Vs{b}", [P, MT, HQ, 32]) for b in range(B)]
            mx = [pb(f"mx{j}", [P, 16]) for j in range(2)]
            neg = [pb(f"neg{j}", [16, P]) for j in range(2)]
            nres = pb("nres", [16, P])
            mparts = [pb(f"mparts{j}", [16, 3, P], BF16) for j in range(2)]
            partk = pb("partk", [P, 3, T], BF16)
        with ExitStack() as phase:
            def pb(name, shape, dt=F32):
                return phase.enter_context(nc.sbuf_tensor(name, shape, dt))

            XH = pb("XH", [P, T], F32R)
            XL = pb("XL", [P, T], F32R)
            CB = [pb(f"CB{j}", [P, T]) for j in range(2)]
            WR = [pb(f"WR{j}", [P, 2, FF]) for j in range(2)]
            WH = [pb(f"WH{j}", [P, 2, FF], F32R) for j in range(2)]
            WL = [pb(f"WL{j}", [P, 2, FF], F32R) for j in range(2)]
            G = [pb(f"G{j}", [P, FC, 512]) for j in range(2)]
            GH = [pb(f"GH{j}", [P, FC, 512], F32R) for j in range(2)]
            GL = [pb(f"GL{j}", [P, FC, 512], F32R) for j in range(2)]
            combT = pb("combT", [E, T])
        with ExitStack() as phase:
            def pb(name, shape, dt=F32):
                return phase.enter_context(nc.sbuf_tensor(name, shape, dt))

            partsb = pb("partsb", [P, 3, T], BF16)
            partkb = pb("partkb", [P, 3, T], BF16)
            V9 = pb("V9", [P, 2, NT, H, VW])
            QB = [pb(f"QB{j}", [P, H, P], BF16) for j in range(2)]
            KB = [pb(f"KB{j}", [P, H, KW], BF16) for j in range(2)]
            VWs = [pb(f"VWs{j}", [P, 2, H, 32]) for j in range(2)]
            PB = [pb(f"PB{j}", [P, HH, P])[:, :, :] for j in range(2)]
            PT = [pb(f"PT{j}", [P, HH, P])[:, :, :] for j in range(2)]
            mxb = pb("mxb", [P, 2, HH])
            Gb = [pb(f"Gb{j}", [P, FC, 512]) for j in range(2)]
            with ExitStack() as early:
                QFb = early.enter_context(nc.sbuf_tensor("QFb", [P, T], F32))
                KFb = early.enter_context(nc.sbuf_tensor("KFb", [P, T], F32))
            OTb = pb("OTb", [P, QUADS, T])

        ps = ctx.enter_context(nc.psum_tensor("ps", [P, 8, 512], F32))
        SB, OB, MB = (0, 1, 2), 3, (4, 6)

        kst = scratch("kst", (H, KR, T), BF16)
        qst = scratch("qst", (H, KR, T), BF16)
        mrow = scratch("mrow", (B, 2, 3, 16, P), BF16)
        kstb = scratch("kstb", (H, KR, B * PADN), BF16)
        qstb = scratch("qstb", (H, KR, T), BF16)
        cst = scratch("cst", (E, T), F32)

        kst_q = kst.rearrange("(q a j) r t -> q j r a t", a=2, j=2)
        qst_q = qst.rearrange("(q a j) r t -> q j r a t", a=2, j=2)

        LN1G, LN1B, LN2G, LN2B, BQ, BKC, B1C = 0, 1, 2, 3, 4, 5, 6

        block = ctx.enter_context(nc.Block())

        def hold(eng, sem, value):
            eng.wait_ge(sem, value)
            eng.nop(nofuse=True)

        NORMS = ("na", "n0", "nb", "nb1", "nb2", "n1")

        def norm_vector(ve, tag, src, dst, ready=None):
            k = NQ * NORMS.index(tag)
            for q in range(NQ):
                if ready is not None:
                    ve.wait_ge(ready, q + 1)
                for t in range(4 * q, 4 * q + 4):
                    ins = nc.vector.bn_stats(st[:, t, :], src[:, t, :])
                ins.then_inc(S("norm_stats"), 1)
                ve.wait_ge(S("norm_stats"), k + q + 1)
                for t in range(4 * q, 4 * q + 4):
                    ins = nc.vector.bn_aggr(mv[:, t, :], st[:, t, :])
                ins.then_inc(S("norm_moments"), 1)
            for t in range(NT):
                if t % 4 == 0:
                    ve.wait_ge(S("norm_rstd"), k + t // 4 + 1)
                nc.vector.tensor_scalar(dst[:, t, :], src[:, t, :], mv[:, t, 0:1], rstd[:, t:t + 1],
                                        ALU.subtract, ALU.mult).then_inc(S(f"{tag}_normed"), 1)

        def norm_gpsimd(g, tag):
            k = NQ * NORMS.index(tag)
            for q in range(NQ):
                c = slice(4 * q, 4 * q + 4)
                g.wait_ge(S("norm_moments"), k + q + 1)
                nc.gpsimd.tensor_scalar(rstd[:, c], mv[:, c, 1], EPS, None, ALU.add).then_inc(S("norm_guarded"), 1)
                g.wait_ge(S("norm_guarded"), k + q + 1)
                nc.gpsimd.tensor_tensor(rstd[:, c], rstd[:, c], mhalf[:, c], ALU.pow).then_inc(S("norm_rstd"), 1)

        def turn_tensor(pe, tag, src, ready):
            for q in range(NQ):
                pe.wait_ge(ready, 4 * q + 4)
                for j in range(4):
                    last = nc.tensor.transpose(ps[:, q, j * P:(j + 1) * P], src[:, 4 * q + j, :], ident[:, :])
                last.then_inc(S(f"{tag}_turned"), 1)

        def turn_scalar(act, tag, dst, gain=None, shift=None):
            for q in (0, 2):
                act.wait_ge(S(f"{tag}_turned"), q + 1)
                d = dst[:, q * QW:(q + 1) * QW]
                if gain is None:
                    nc.scalar.activation(d, ps[:, q, :], ACT.Copy).then_inc(S(f"{tag}_even"), 1)
                else:
                    nc.scalar.activation(d, ps[:, q, :], ACT.Identity, bias=shift, scale=gain).then_inc(S(f"{tag}_even"), 1)

        def turn_vector(ve, tag, dst, gain=None, shift=None):
            for q in (1, 3):
                ve.wait_ge(S(f"{tag}_turned"), q + 1)
                d = dst[:, q * QW:(q + 1) * QW]
                if gain is None:
                    nc.vector.tensor_copy(d, ps[:, q, :]).then_inc(S(f"{tag}_odd"), 1)
                else:
                    nc.vector.tensor_scalar(d, ps[:, q, :], gain, shift, ALU.mult, ALU.add).then_inc(S(f"{tag}_odd"), 1)

        def turned_wait(eng, tag, q):
            eng.wait_ge(S(f"{tag}_odd" if q % 2 else f"{tag}_even"), q // 2 + 1)

        def split_vector(ve, tag, src, parts, b):
            c = slice(b * N, (b + 1) * N)
            done = S(f"{tag}_split")
            res = HN[:, :, :].rearrange("p t c -> p (t c)")
            nc.vector.tensor_copy(parts[:, 0, c], src[:, c]).then_inc(done, 1)
            ve.wait_ge(done, 4 * b + 1)
            nc.vector.tensor_tensor(res[:, c], src[:, c], parts[:, 0, c], ALU.subtract).then_inc(done, 1)
            ve.wait_ge(done, 4 * b + 2)
            nc.vector.tensor_copy(parts[:, 1, c], res[:, c]).then_inc(done, 1)
            ve.wait_ge(done, 4 * b + 3)
            nc.vector.tensor_tensor(parts[:, 2, c], res[:, c], parts[:, 1, c], ALU.subtract).then_inc(done, 1)

        def stack_sync(sp, tag, parts, dst, order, b, at):
            sp.wait_ge(S(f"{tag}_split"), 4 * b + 4)
            rows = dst.rearrange("h (r d) t -> r h d t", r=NR)
            for r, part in enumerate(order):
                sp.dma_start(rows[r, :, :, at:at + N], parts[:, part, b * N:(b + 1) * N])\
                  .then_inc(S(f"{tag}_stacked{b}"), 16)

        def qk_tensor(pe, tag, w, turned):
            for q in range(NQ):
                turned_wait(pe, turned, q)
                for which in range(2):
                    nc.tensor.matmul(ps[:, 4 * which + q, :], w[:, which * P:(which + 1) * P],
                                     XT[:, q * QW:(q + 1) * QW], start=True, stop=True).then_inc(S(f"{tag}_qk"), 1)

        def v_tensor(pe, tag, w):
            for q in range(NQ):
                pe.wait_ge(S(f"{tag}_q_out"), q + 1)
                for j in range(4):
                    t = 4 * q + j
                    last = nc.tensor.matmul(ps[:, q, j * P:(j + 1) * P], XT[:, t * P:(t + 1) * P], w[:, 2 * P:3 * P],
                                            start=True, stop=True)
                last.then_inc(S(f"{tag}_v"), 1)

        def head_norm_vector(ve, r):
            for t in range(NT):
                ve.wait_ge(S("o_turned"), NT * r + t + 1)
                o = ps[:, t % 4, :].rearrange("p (h c) -> p h c", h=H)
                nc.vector.reciprocal(rsa[:, t, :], o[:, :, D]).then_inc(S("rs_ready"), 1)
                ve.wait_ge(S("rs_ready"), NT * r + t + 1)
                nc.vector.tensor_tensor(HN[:, t, :].rearrange("p (h d) -> p h d", h=H), o[:, :, 0:D],
                                        rsa[:, t, :].unsqueeze(2).broadcast_to([P, H, D]), ALU.mult)\
                  .then_inc(S("o_normed"), 1)

        def head_back_scalar(act, r):
            for q in range(NQ):
                act.wait_ge(S("head_back"), NQ * r + q + 1)
                nc.scalar.activation(XT[:, q * QW:(q + 1) * QW], ps[:, 4 + q % 2, :], ACT.Copy).then_inc(S("head_xt"), 1)

        def head_project_tensor(pe, r, src, w, added):
            for s in range(NQ + 2):
                if s < NQ:
                    for t in range(4 * s, 4 * s + 4):
                        if t >= 4:
                            pe.wait_ge(S("o_normed"), NT * r + t - 3)
                        for quad in range(QUADS):
                            ins = nc.tensor.transpose(ps[:, t % 4, quad * P:(quad + 1) * P],
                                                      src[:, quad, t * P:(t + 1) * P], ident[:, :])
                        ins.then_inc(S("o_turned"), 1)
                if 1 <= s <= NQ:
                    q = s - 1
                    pe.wait_ge(S("o_normed"), NT * r + 4 * q + 4)
                    if q >= 2:
                        pe.wait_ge(S("head_xt"), NQ * r + q - 1)
                    for j in range(4):
                        ins = nc.tensor.transpose(ps[:, 4 + q % 2, j * P:(j + 1) * P], HN[:, 4 * q + j, :], ident[:, :])
                    ins.then_inc(S("head_back"), 1)
                if s >= 2:
                    q = s - 2
                    pe.wait_ge(S("head_xt"), NQ * r + q + 1)
                    if q >= 2:
                        pe.wait_ge(added, q - 1)
                    for j in range(4):
                        t = 4 * q + j
                        ins = nc.tensor.matmul(ps[:, 6 + q % 2, j * P:(j + 1) * P], XT[:, t * P:(t + 1) * P], w[:, :],
                                               start=True, stop=True)
                    ins.then_inc(S("head_proj"), 1)

        def expert_in_scalar(act, m):
            for q in range(NQ):
                act.wait_ge(S(f"{m}_turned"), q + 1)
                nc.scalar.activation(XT[:, q * QW:(q + 1) * QW], ps[:, q, :], ACT.Copy).then_inc(S(f"{m}_xt"), 1)

        def expert_in_vector(ve, m):
            for q in range(NQ):
                c = slice(q * QW, (q + 1) * QW)
                ve.wait_ge(S(f"{m}_xt"), q + 1)
                nc.vector.tensor_copy(XH[:, c], XT[:, c]).then_inc(S(f"{m}_xh"), 1)
                ve.wait_ge(S(f"{m}_xh"), q + 1)
                nc.vector.tensor_tensor(XL[:, c], XT[:, c], XH[:, c], ALU.subtract).then_inc(S(f"{m}_xl"), 1)

        def route_tensor(pe, m, src, normed):
            for q in range(NQ + 1):
                if q < NQ:
                    pe.wait_ge(normed, 4 * q + 4)
                    for j in range(4):
                        last = nc.tensor.transpose(ps[:, q, j * P:(j + 1) * P], src[:, 4 * q + j, :], ident[:, :])
                    last.then_inc(S(f"{m}_turned"), 1)
                if q:
                    pe.wait_ge(S(f"{m}_xt"), q)
                    for t in range(4 * q - 4, 4 * q):
                        last = nc.tensor.matmul(ps[:, 4, t * E:(t + 1) * E], XT[:, t * P:(t + 1) * P], rw[:, :],
                                                start=True, stop=True)
            last.then_inc(S(f"{m}_logits"), 1)

        def route_vector(ve, m):
            done = S(f"{m}_route")
            n = [0]

            def step(ins):
                n[0] += 1
                ins.then_inc(done, 1)
                ve.wait_ge(done, n[0])

            ve.wait_ge(S(f"{m}_logits"), 1)
            step(nc.vector.tensor_copy(L[:, :, :].rearrange("p t e -> p (t e)"), ps[:, 4, 0:NT * E]))
            mine = L[:, :, :].unsqueeze(3).broadcast_to([P, NT, E, E])
            theirs = L[:, :, :].unsqueeze(2).broadcast_to([P, NT, E, E])
            step(nc.vector.tensor_tensor(ties[:, :, :, :], theirs, mine, ALU.is_equal))
            step(nc.vector.tensor_tensor(ties[:, :, :, :], ties[:, :, :, :],
                                         tri[:, :, :].unsqueeze(1).broadcast_to([P, NT, E, E]), ALU.mult))
            step(nc.vector.tensor_tensor(beats[:, :, :, :], theirs, mine, ALU.is_gt))
            step(nc.vector.tensor_tensor(beats[:, :, :, :], beats[:, :, :, :], ties[:, :, :, :], ALU.add))
            step(nc.vector.tensor_reduce(rank[:, :, :], beats[:, :, :, :], AX, ALU.add))
            step(nc.vector.tensor_reduce(lmax[:, :], L[:, :, :], AX, ALU.max))
            step(nc.vector.tensor_tensor(L[:, :, :], L[:, :, :], lmax[:, :].unsqueeze(2).broadcast_to([P, NT, E]),
                                         ALU.subtract))
            ve.wait_ge(S(f"{m}_exps"), 1)
            step(nc.vector.tensor_scalar(rank[:, :, :], rank[:, :, :], 2.0, None, ALU.is_lt))
            step(nc.vector.tensor_tensor(comb[:, :, :], comb[:, :, :], rank[:, :, :], ALU.mult))
            step(nc.vector.tensor_reduce(lmax[:, :], comb[:, :, :], AX, ALU.add))
            step(nc.vector.reciprocal(lmax[:, :], lmax[:, :]))
            nc.vector.tensor_tensor(comb[:, :, :], comb[:, :, :], lmax[:, :].unsqueeze(2).broadcast_to([P, NT, E]),
                                    ALU.mult).then_inc(S(f"{m}_comb"), 1)

        def route_scalar(act, m):
            act.wait_ge(S(f"{m}_route"), 8)
            nc.scalar.activation(comb[:, :, :], L[:, :, :], ACT.Exp).then_inc(S(f"{m}_exps"), 1)

        def comb_tensor(pe, m):
            pe.wait_ge(S(f"{m}_comb"), 1)
            for t in range(NT):
                last = nc.tensor.transpose(ps[0:E, 4 + t // 4, (t % 4) * P:(t % 4 + 1) * P], comb[:, t, :], ident[:, :])
            last.then_inc(S(f"{m}_combT"), 1)

        def comb_bias(pe, m):
            pe.wait_ge(S(f"{m}_combT_out"), 1)
            for q in range(NQ):
                nc.tensor.matmul(ps[:, 4 + q, :], b2e[:, :], combT[:, q * QW:(q + 1) * QW], start=True, stop=False)

        def comb_vector(ve, m):
            ve.wait_ge(S(f"{m}_combT"), 1)
            nc.vector.tensor_copy(combT[:, :], ps[0:E, 4:8, :].rearrange("p a n -> p (a n)")).then_inc(S(f"{m}_combT_out"), 1)

        def up(i, s):
            p, q = s // 4 % 2, s % 4
            for f in range(FC):
                w = slice(f * P, (f + 1) * P)
                nc.tensor.wait_ge(S("gelu_out"), 32 * i + 4 * s + f + 1)
                for n, (a, x) in enumerate(((WH, XH), (WH, XL), (WL, XH))):
                    ins = nc.tensor.matmul(ps[:, f, :], a[p][:, 0, w], x[:, q * QW:(q + 1) * QW],
                                           start=(n == 0), stop=(n == 2))
                ins.then_inc(S("up_done"), 1)

        def down(i, s, last):
            p, q = s // 4, s % 4
            for f in range(FC):
                if f % 2 == 0:
                    nc.tensor.wait_ge(S("halved"), 4 + 16 * i + 2 * s + f // 2 + 1)
                w = slice(f * P, (f + 1) * P)
                for n, (a, g) in enumerate(((WH, GH), (WH, GL), (WL, GH))):
                    ins = nc.tensor.matmul(ps[:, 4 + q, :], a[p][:, 1, w], g[s % 2][:, f, :], start=False,
                                           stop=(last and s >= 4 and f == FC - 1 and n == 2))
            ins.then_inc(S("down_done"), 1)

        def experts_tensor(pe, m, r):
            def body(i, last):
                for s in range(8):
                    if not (last and s >= 6):
                        if s in (2, 6):
                            pe.wait_ge(S("w_halved"), 4 * i + 2 * (s // 4 + 1) + 6)
                        up(i, s + 2)
                    down(i, s, last)

            pe.wait_ge(S(f"{m}_xl"), NQ)
            pe.wait_ge(S("w_halved"), 16 * r + 6)
            up(4 * r, 0)
            comb_tensor(pe, m)
            up(4 * r, 1)
            comb_bias(pe, m)
            with pe.Fori(4 * r, 4 * r + 3) as i:
                body(i, False)
            body(4 * r + 3, True)
            for q in range(NQ):
                pe.wait_ge(S(f"{m}_y_odd" if q % 2 else f"{m}_y_even"), q // 2 + 1)
                for j in range(4):
                    t = 4 * q + j
                    ins = nc.tensor.transpose(ps[:, q, j * P:(j + 1) * P], XT[:, t * P:(t + 1) * P], ident[:, :])
                ins.then_inc(S(f"{m}_y_turned"), 1)

        def experts_scalar(act, m, r):
            def gelu(i, s, f):
                act.wait_ge(S("up_done"), 32 * i + 4 * s + f + 1)
                if f == 0:
                    act.wait_ge(S("halved"), 16 * i + 2 * s + 2)
                nc.scalar.activation(G[s % 2][:, f, :], ps[:, f, :], ACT.Gelu,
                                     bias=b1s[:, s // 4 % 2, f:f + 1]).then_inc(S("gelu_out"), 1)

            def high(i, s, half):
                act.wait_ge(S("weighted"), 16 + 16 * i + 2 * s + half + 1)
                act.wait_ge(S("down_done"), 8 * i + s + 7)
                c = slice(2 * half, 2 * half + 2)
                nc.scalar.activation(GH[s % 2][:, c, :], G[s % 2][:, c, :], ACT.Copy).then_inc(S("rounded"), 1)

            def body(i, last):
                for s in range(8):
                    more = not (last and s == 7)
                    if more:
                        if s in (3, 7):
                            act.wait_ge(S("b1_in"), 2 * i + s // 4 + 2)
                        gelu(i, s + 1, 0)
                        gelu(i, s + 1, 1)
                    high(i, s, 1)
                    if more:
                        gelu(i, s + 1, 2)
                        gelu(i, s + 1, 3)
                        high(i, s + 1, 0)

            act.wait_ge(S("b1_in"), 8 * r + 1)
            for f in range(FC):
                gelu(4 * r, 0, f)
            high(4 * r, 0, 0)
            with act.Fori(4 * r, 4 * r + 3) as i:
                body(i, False)
            body(4 * r + 3, True)
            for q in (0, 2):
                act.wait_ge(S("down_done"), 8 + 32 * (r + 1) - 3 + q)
                nc.scalar.activation(XT[:, q * QW:(q + 1) * QW], ps[:, 4 + q, :], ACT.Copy).then_inc(S(f"{m}_y_even"), 1)

        def experts_vector(ve, m, r):
            def weigh(i, s, half):
                p, q = s // 4 % 2, s % 4
                ve.wait_ge(S("gelu_out"), 4 + 32 * i + 4 * s + 2 * half + 2)
                g = G[s % 2][:, 2 * half:2 * half + 2, :]
                nc.vector.tensor_tensor(g, g, CB[p][:, q * QW:(q + 1) * QW].unsqueeze(1).broadcast_to([P, 2, QW]),
                                        ALU.mult).then_inc(S("weighted"), 1)

            def low(i, s, half):
                ve.wait_ge(S("rounded"), 16 * i + 2 * s + half + 1)
                c = slice(2 * half, 2 * half + 2)
                nc.vector.tensor_tensor(GL[s % 2][:, c, :], G[s % 2][:, c, :], GH[s % 2][:, c, :],
                                        ALU.subtract).then_inc(S("halved"), 1)

            def body(i, last):
                for s in range(8):
                    more = not (last and s == 7)
                    if more:
                        if s in (3, 7):
                            ve.wait_ge(S(f"cb_in{(s // 4 + 1) % 2}"), 16 * i + (32 if s == 7 else 16))
                        weigh(i, s + 1, 0)
                    low(i, s, 1)
                    if more:
                        weigh(i, s + 1, 1)
                        low(i, s + 1, 0)

            ve.wait_ge(S("cb_in0"), 64 * r + 16)
            weigh(4 * r, 0, 0)
            weigh(4 * r, 0, 1)
            low(4 * r, 0, 0)
            with ve.Fori(4 * r, 4 * r + 3) as i:
                body(i, False)
            body(4 * r + 3, True)
            for q in (1, 3):
                ve.wait_ge(S("down_done"), 8 + 32 * (r + 1) - 3 + q)
                nc.vector.tensor_copy(XT[:, q * QW:(q + 1) * QW], ps[:, 4 + q, :]).then_inc(S(f"{m}_y_odd"), 1)
            for q in range(NQ):
                ve.wait_ge(S(f"{m}_y_turned"), q + 1)
                xq = X[:, 4 * q:4 * q + 4, :].rearrange("p t c -> p (t c)")
                nc.vector.tensor_tensor(xq, xq, ps[:, q, :], ALU.add).then_inc(S(f"{m}_x"), 1)

        def experts_gpsimd(g, m, r):
            def expert(i, p):
                hold(g, S("down_done"), 8 * i + 4 * p + 4)
                e = 2 * (i - 4 * r) + p
                nc.gpsimd.tensor_copy(b1s[:, p, :].unsqueeze(1), b1e[:, bass.ds(e, 1), :]).then_inc(S("b1_in"), 1)
                hold(g, S(f"w_in{p}"), 32 * i + 32)
                nc.gpsimd.tensor_copy(WH[p][:, :, :], WR[p][:, :, :]).then_inc(S("w_halved"), 1)
                hold(g, S("w_halved"), 4 * i + 2 * p + 5)
                nc.gpsimd.tensor_tensor(WL[p][:, :, :], WR[p][:, :, :], WH[p][:, :, :], ALU.subtract)\
                  .then_inc(S("w_halved"), 1)

            with g.Fori(4 * r, 4 * r + 4) as i:
                expert(i, 0)
                expert(i, 1)

        def experts_sync(sp, m, r, ready):
            def weights(i, p):
                hold(sp, S("w_halved"), 4 * i + 2 * p + 2)
                e = 2 * (i - 4 * r) + p
                sp.dma_start(WR[p][:, 0:1, :], dram["ffn_w1"][bass.ds(e, 1), :, :].rearrange("e p f -> p e f"))\
                  .then_inc(S(f"w_in{p}"), 16)
                sp.dma_start(WR[p][:, 1:2, :], dram["ffn_w2"][bass.ds(e, 1), :, :].rearrange("e p f -> p e f"))\
                  .then_inc(S(f"w_in{p}"), 16)

            def combines(i, p):
                hold(sp, S("weighted"), 16 * i + 8 * p + 8)
                e = 2 * (i - 4 * r) + p
                sp.dma_start(CB[p][:, :], cst[bass.ds(e, 1), :].broadcast_to([P, T])).then_inc(S(f"cb_in{p}"), 16)

            ready(sp)
            weights(4 * r, 0)
            weights(4 * r, 1)
            sp.wait_ge(S(f"{m}_combT_out"), 1)
            sp.dma_start(cst, combT[:, :]).then_inc(S("cst_out"), 16)
            sp.wait_ge(S("cst_out"), 16 * (r + 1))
            combines(4 * r, 0)
            combines(4 * r, 1)
            with sp.Fori(4 * r + 1, 4 * r + 4) as i:
                for p in range(2):
                    weights(i, p)
                    combines(i, p)

        @block.sync
        def _(sp):
            for name, dst in (("wqkva", wqkva), ("ident", ident), ("wpa", wpa), ("bpa", bpa),
                              ("wqkvb", wqkvb), ("colb", colb), ("bvb", bvb), ("bob", bob), ("b2b", b2b),
                              ("wob", wob), ("w1b", w1b), ("w2b", w2b), ("rw", rw), ("b1e", b1e), ("b2e", b2e),
                              ("tri", tri), ("causal", causal), ("identb", identb)):
                ap = dst[tuple(slice(None) for _ in dst.shape)]
                sp.dma_start(ap, dram[name]).then_inc(S("consts_in"), 16)
            def load(i, b):
                for j in range(2):
                    sp.dma_start(KA[b][KR * j:KR * j + KR, :, :], kst_q[i, j, :, :, b * N:(b + 1) * N])\
                      .then_inc(S(f"kq_in{b}"), 16)
                    sp.dma_start(QZ[b][KR * j:KR * j + KR, :, j, :], qst_q[i, j, :, :, b * N:(b + 1) * N])\
                      .then_inc(S(f"kq_in{b}"), 16)

            for b in range(B):
                stack_sync(sp, "aq", parts, qst, Q_PARTS, b, b * N)
                stack_sync(sp, "ak", partk, kst, K_PARTS, b, b * N)
                sp.wait_ge(S(f"aq_stacked{b}"), 16 * NR)
                sp.wait_ge(S(f"ak_stacked{b}"), 16 * NR)
                if b == 0:
                    sp.wait_ge(S("qz_clear"), 4)
                load(0, b)
            with sp.Fori(0, QUADS - 1) as i:
                for b in range(B):
                    hold(sp, S("exp_done"), 128 * i + 64 * b + 128)
                    load(i + 1, b)
            experts_sync(sp, "m0", 0, lambda sp: sp.wait_ge(S("x1"), NQ))
            sp.wait_ge(S("zero_ready"), 1)
            for b in range(B):
                sp.dma_start(kstb[:, :, b * PADN:b * PADN + BK].rearrange("h r t -> (h r) t")
                             .rearrange("(p g) t -> p g t", g=H * KR // P),
                             zer[:, 0:BK].unsqueeze(1).broadcast_to([P, H * KR // P, BK])).then_inc(S("b_pads"), 16)
            for b in range(B):
                sp.wait_ge(S("b_v_out"), 2 * b + 2)
                sp.dma_start(V9[BK:P, 0, b * MT:(b + 1) * MT, :, :], V9[0:BK, 1, b * MT:(b + 1) * MT, :, :])\
                  .then_inc(S("bv_moved"), 16)
                sp.dma_start(V9[0:BK, 0, b * MT + 1:(b + 1) * MT, :, :], V9[BK:P, 1, b * MT:(b + 1) * MT - 1, :, :])\
                  .then_inc(S("bv_moved"), 16)
                stack_sync(sp, "bq", partsb, qstb, Q_PARTS, b, b * N)
                stack_sync(sp, "bk", partkb, kstb, K_PARTS, b, b * PADN + BK)
            sp.wait_ge(S("b_pads"), 16 * B)
            for b in range(B):
                sp.wait_ge(S(f"bq_stacked{b}"), 16 * NR)
                sp.wait_ge(S(f"bk_stacked{b}"), 16 * NR)
                with sp.Fori(b * MT // 2, (b + 1) * MT // 2) as i:
                    for j in range(2):
                        at = 2 * P * i + j * P
                        pad = at + BK * b
                        u = 4 * i + 2 * j
                        hold(sp, S("b_scores"), u + 2)
                        sp.dma_start(QB[j][0:KR, :, :], qstb[:, :, bass.ds(at, P)].rearrange("h r t -> r h t"))\
                          .then_inc(S(f"b_qk_in{j}"), 16)
                        sp.dma_start(KB[j][0:KR, :, :], kstb[:, :, bass.ds(pad, KW)].rearrange("h r t -> r h t"))\
                          .then_inc(S(f"b_qk_in{j}"), 16)
            experts_sync(sp, "m1", 1, lambda sp: sp.wait_ge(S("x3"), NQ))
            sp.wait_ge(S("m1_x"), NQ)
            sp.dma_start(out.rearrange("b (t p) c -> p (b t) c", p=P), X[:, :, :]).then_inc(S("stored"), 16)
            sp.wait_ge(S("stored"), 16)

        @block.gpsimd
        def _(g):
            g.nop().then_inc(S("w_halved"), 4)
            nc.gpsimd.memset(mhalf[:, :], -0.5).then_inc(S("half_ready"), 1)
            g.wait_ge(S("half_ready"), 1)
            norm_gpsimd(g, "na")
            for b in range(B):
                nc.gpsimd.memset(QZ[b][:, :, :, :], 0.0).then_inc(S("qz_clear"), 1)
                nc.gpsimd.memset(KA[b][:, :, :], 1.0).then_inc(S("qz_clear"), 1)
                nc.gpsimd.memset(Vs[b][:, :, :, :], 0.0).then_inc(S("vs_set"), 1)
                g.wait_ge(S("vs_set"), 2 * b + 1)
                nc.gpsimd.memset(Vs[b][:, :, :, D:D + 1], 1.0).then_inc(S("vs_set"), 1)
            g.wait_ge(S("na_normed"), NT)
            g.wait_ge(S("consts_in"), 16 * 18)
            nc.gpsimd.tensor_tensor(X[:, :, :], X[:, :, :], bpa[:, :].unsqueeze(1).broadcast_to([P, NT, P]),
                                    ALU.add).then_inc(S("x_biased"), 1)
            g.wait_ge(S("vs_set"), 4)
            g.wait_ge(S("a_v_out"), NQ)

            def values(i, b):
                nc.gpsimd.tensor_copy(Vs[b][:, :, :, 0:D],
                                      Vn[:, bass.ds(B * i + b, 1), :, :].rearrange("p o m (h d) -> p (o m) h d", h=HQ))\
                  .then_inc(S("vs_in"), 1)

            def max_rows(i, b, nh):
                c = B * i + b
                hold(g, S("max_done"), ITEMS * c + TURN_AT[nh] + 1)
                q = S("msplit")
                k = 8 * c + 4 * nh
                nc.gpsimd.tensor_copy(mparts[nh][:, 0, :], neg[nh][:, :]).then_inc(q, 1)
                hold(g, q, k + 1)
                nc.gpsimd.tensor_tensor(nres[:, :], neg[nh][:, :], mparts[nh][:, 0, :], ALU.subtract).then_inc(q, 1)
                hold(g, q, k + 2)
                nc.gpsimd.tensor_copy(mparts[nh][:, 1, :], nres[:, :]).then_inc(q, 1)
                hold(g, q, k + 3)
                nc.gpsimd.tensor_tensor(mparts[nh][:, 2, :], nres[:, :], mparts[nh][:, 1, :], ALU.subtract).then_inc(q, 1)
                hold(g, q, k + 4)
                g.dma_start(mrow[b, nh].rearrange("s c n -> c s n"), mparts[nh][:, :, :]).then_inc(S(f"mrow_out{nh}"), 16)
                hold(g, S(f"mrow_out{nh}"), 16 * c + 16)
                g.dma_start(QZ[b][96:99, :, :, nh * 512:(nh + 1) * 512].rearrange("s a j n -> s (a j) n"),
                            mrow[b, nh].rearrange("s (h t) n -> s h (t n)", h=HQ)).then_inc(S(f"mrow_in{b}{nh}"), 16)

            max_rows(0, 0, 0)
            values(0, 0)
            values(0, 1)

            def follow(i, b, last):
                max_rows(i, b, 1)
                if not (last and b == 1):
                    max_rows(i + b, 1 - b, 0)
                if not last:
                    hold(g, S("pv_done"), 2 + 32 * i + 16 * b + 16)
                    values(i + 1, b)

            with g.Fori(0, QUADS - 1) as i:
                for b in range(B):
                    follow(i, b, False)
            for b in range(B):
                follow(QUADS - 1, b, True)
            norm_gpsimd(g, "n0")
            experts_gpsimd(g, "m0", 0)
            norm_gpsimd(g, "nb")
            norm_gpsimd(g, "nb1")
            nc.gpsimd.memset(zer[:, :], 0.0).then_inc(S("zero_ready"), 1)
            for b in range(B):
                nc.gpsimd.memset(V9[0:BK, 0, b * MT, :, :], 0.0).then_inc(S("v9_zero"), 1)
            nc.gpsimd.memset(V9[:, 1, :, :, D:D + 1], 1.0).then_inc(S("v9_ones"), 1)
            for j in range(2):
                nc.gpsimd.memset(VWs[j][:, :, :, :], 0.0).then_inc(S("vws_zero"), 1)
            g.wait_ge(S("v9_zero"), B)
            for b in range(B):
                nc.gpsimd.memset(V9[0:BK, 0, b * MT, :, D:D + 1], 1.0).then_inc(S("v9_zero"), 1)
            g.wait_ge(S("nb1_normed"), NT)
            nc.gpsimd.tensor_tensor(XN[:, :, :], XN[:, :, :], bob[:, :].unsqueeze(1).broadcast_to([P, NT, P]),
                                    ALU.add).then_inc(S("xn_biased"), 1)
            g.wait_ge(S("b_v_out"), NQ)
            g.wait_ge(S("bv_moved"), 16 * 2 * B)
            g.wait_ge(S("v9_zero"), 2 * B)
            g.wait_ge(S("vws_zero"), 2)
            with g.Fori(0, NT // 2) as i:
                for j in range(2):
                    hold(g, S("b_pv"), 4 * i + 2 * j + 2)
                    nc.gpsimd.tensor_copy(VWs[j][:, :, :, 0:VW].rearrange("p w h c -> p w h c"),
                                          V9[:, :, bass.ds(2 * i + j, 1), :, :].rearrange("p w t h c -> p (w t) h c"))\
                      .then_inc(S(f"b_v_in{j}"), 1)
            norm_gpsimd(g, "nb2")
            g.wait_ge(S("nb2_normed"), NT)
            nc.gpsimd.tensor_tensor(XN[:, :, :], XN[:, :, :], b2b[:, :].unsqueeze(1).broadcast_to([P, NT, P]),
                                    ALU.add).then_inc(S("xn_biased"), 1)
            g.wait_ge(S("xn_biased"), 2)
            nc.gpsimd.tensor_tensor(X[:, :, :], X[:, :, :], XN[:, :, :], ALU.add).then_inc(S("x_plus"), 1)
            norm_gpsimd(g, "n1")
            experts_gpsimd(g, "m1", 1)

        @block.scalar
        def _(act):
            act.dma_start(X[:, :, :], dram["x"].rearrange("b (t p) c -> p (b t) c", p=P)).then_inc(S("x_in"), 16)
            act.nop().then_inc(S("exp_done"), 64)
            act.nop().then_inc(S("gelu_out"), 4)
            turn_scalar(act, "na", XT)

            for q in range(NQ):
                act.wait_ge(S("a_qk"), 2 * q + 1)
                nc.scalar.activation(QF[:, q * QW:(q + 1) * QW], ps[:, q, :], ACT.Copy, scale=SCALE).then_inc(S("a_q_out"), 1)
                act.wait_ge(S("a_qk"), 2 * q + 2)
                nc.scalar.activation(KF[:, q * QW:(q + 1) * QW], ps[:, 4 + q, :], ACT.Copy).then_inc(S("a_k_out"), 1)
            for q in range(NQ):
                act.wait_ge(S("a_v"), q + 1)
                b, m = q // 2, q % 2
                for quad in range(QUADS):
                    ins = nc.scalar.activation(
                        Vn[:, B * quad + b, 4 * m:4 * m + 4, :],
                        ps[:, q, :].rearrange("p (m c) -> p m c", m=4)[:, :, 32 * quad:32 * quad + 32], ACT.Copy)
                ins.then_inc(S("a_v_out"), 1)

            def unit(i, b, u):
                for h in range(HQ):
                    k = 4 * u + h
                    act.wait_ge(S("s_full"), 128 * i + 64 * b + k + 1)
                    if h == 0:
                        act.wait_ge(S("pv_done"), 32 * i + 16 * b + u + 1)
                    nc.scalar.activation(EX[u % 2][:, h, :], ps[:, SB[k % 3], :], ACT.Exp).then_inc(S("exp_done"), 1)

            def output(i, b, nh):
                act.wait_ge(S("pv_done"), 2 + 32 * i + 16 * b + 8 * nh + 8)
                nc.scalar.activation(OT[:, bass.ds(i, 1), b * N + nh * 512:b * N + (nh + 1) * 512],
                                     ps[:, OB, :].unsqueeze(1), ACT.Copy).then_inc(S("o_out"), 1)

            def combination(i, b, more):
                for u in range(1, UNITS):
                    unit(i, b, u)
                    if u == MT:
                        output(i, b, 0)
                if more:
                    unit(i + b, 1 - b, 0)
                output(i, b, 1)

            unit(0, 0, 0)
            with act.Fori(0, QUADS - 1) as i:
                combination(i, 0, True)
                combination(i, 1, True)
            combination(QUADS - 1, 0, True)
            combination(QUADS - 1, 1, False)

            head_back_scalar(act, 0)
            expert_in_scalar(act, "m0")
            route_scalar(act, "m0")
            experts_scalar(act, "m0", 0)
            turn_scalar(act, "b1", XT, colb[:, LN1G:LN1G + 1], colb[:, LN1B:LN1B + 1])
            for q in range(NQ):
                act.wait_ge(S("b_qk"), 2 * q + 2)
                nc.scalar.activation(KFb[:, q * QW:(q + 1) * QW], ps[:, 4 + q, :], ACT.Identity,
                                     bias=colb[:, BKC:BKC + 1]).then_inc(S("b_k_out"), 1)

            def b_exp(u, j):
                act.wait_ge(S("b_shifted"), u + 1)
                nc.scalar.activation(PB[j], PB[j], ACT.Exp).then_inc(S("b_exp"), 1)

            def b_scalar(i, last=False):
                for k in range(4):
                    u, j = 4 * i + k, k % 2
                    if not (last and k == 3):
                        b_exp(u + 1, 1 - j)
                    act.wait_ge(S("b_pturned"), u + 1)
                    act.wait_ge(S("b_pv"), u + 4 - 1)
                    nc.scalar.activation(PT[j], ps[:, 4 + 2 * j:6 + 2 * j, :].rearrange("p a (h n) -> p (a h) n", h=4),
                                         ACT.Copy).then_inc(S("b_pt"), 1)

            b_exp(0, 0)
            with act.Fori(0, BU // 4 - 1) as i:
                b_scalar(i)
            b_scalar(BU // 4 - 1, last=True)
            head_back_scalar(act, 1)
            turn_scalar(act, "b2", XT, colb[:, LN2G:LN2G + 1], colb[:, LN2B:LN2B + 1])
            for s in range(NQ):
                for f in range(FC):
                    act.wait_ge(S("mlp_up"), 4 * s + f + 1)
                    if f == 0 and s >= 2:
                        act.wait_ge(S("mlp_down"), s - 1)
                    nc.scalar.activation(Gb[s % 2][:, f, :], ps[:, f, :], ACT.Gelu,
                                         bias=colb[:, B1C + f:B1C + f + 1]).then_inc(S("mlp_gelu"), 1)
            expert_in_scalar(act, "m1")
            route_scalar(act, "m1")
            experts_scalar(act, "m1", 1)

        @block.vector
        def _(ve):
            ve.nop().then_inc(S("weighted"), 16)
            ve.nop().then_inc(S("halved"), 4)
            ve.wait_ge(S("x_in"), 16)
            norm_vector(ve, "na", X, XN)
            turn_vector(ve, "na", XT)
            for b in range(B):
                ve.wait_ge(S("a_q_out"), 2 * b + 2)
                split_vector(ve, "aq", QF, parts, b)
                ve.wait_ge(S("aq_split"), 4 * b + 4)
                ve.wait_ge(S("a_k_out"), 2 * b + 2)
                split_vector(ve, "ak", KF, partk, b)
                ve.wait_ge(S("ak_split"), 4 * b + 4)

            def maxima(i, b):
                c = B * i + b
                for k, item in enumerate(ITEM_LIST):
                    ve.wait_ge(S("max_full"), ITEMS * c + k + 1)
                    nh = item[1]
                    if item[0] == "max":
                        _, _, h, nt = item
                        nc.vector.tensor_reduce(mx[nh][:, 4 * h + nt:4 * h + nt + 1],
                                                ps[:, MB[k % 2]:MB[k % 2] + 2, :].rearrange("p a n -> p (a n)"), AX, ALU.max)\
                          .then_inc(S("max_done"), 1)
                    else:
                        if not (isinstance(c, int) and c == 0):
                            ve.wait_ge(S("msplit"), 8 * c - 8 + 4 * nh + 4)
                        nc.vector.tensor_scalar(neg[nh][:, :], ps[0:16, MB[k % 2], 0:P], -1.0, None, ALU.mult)\
                          .then_inc(S("max_done"), 1)

            maxima(0, 0)
            with ve.Fori(0, QUADS - 1) as i:
                maxima(i, 1)
                maxima(i + 1, 0)
            maxima(QUADS - 1, 1)
            head_norm_vector(ve, 0)
            ve.wait_ge(S("x_biased"), 1)
            for q in range(NQ):
                ve.wait_ge(S("head_proj"), q + 1)
                xq = X[:, 4 * q:4 * q + 4, :].rearrange("p t c -> p (t c)")
                nc.vector.tensor_tensor(xq, xq, ps[:, 6 + q % 2, :], ALU.add).then_inc(S("x1"), 1)
            norm_vector(ve, "n0", X, XN, S("x1"))
            expert_in_vector(ve, "m0")
            route_vector(ve, "m0")
            comb_vector(ve, "m0")
            experts_vector(ve, "m0", 0)
            norm_vector(ve, "nb", X, XN, S("m0_x"))
            ve.wait_ge(S("nb_normed"), NT)
            norm_vector(ve, "nb1", XN, HN)
            turn_vector(ve, "b1", XT, colb[:, LN1G:LN1G + 1], colb[:, LN1B:LN1B + 1])
            for q in range(NQ):
                ve.wait_ge(S("b_qk"), 2 * q + 1)
                nc.vector.tensor_scalar(QFb[:, q * QW:(q + 1) * QW], ps[:, q, :], colb[:, BQ:BQ + 1], SCALE,
                                        ALU.add, ALU.mult).then_inc(S("b_q_out"), 1)
            ve.wait_ge(S("v9_ones"), 1)
            for q in range(NQ):
                ve.wait_ge(S("b_v"), q + 1)
                for j in range(4):
                    t = 4 * q + j
                    ins = nc.vector.tensor_tensor(V9[:, 1, t, :, 0:D],
                                                  ps[:, q, j * P:(j + 1) * P].rearrange("p (h d) -> p h d", h=H),
                                                  bvb[:, :].rearrange("p (h d) -> p h d", h=H), ALU.add)
                ins.then_inc(S("b_v_out"), 1)
            ve.wait_ge(S("b_q_out"), NQ)
            for b in range(B):
                split_vector(ve, "bq", QFb, partsb, b)
                ve.wait_ge(S("bq_split"), 4 * b + 4)
                ve.wait_ge(S("b_k_out"), 2 * b + 2)
                split_vector(ve, "bk", KFb, partkb, b)
                ve.wait_ge(S("bk_split"), 4 * b + 4)

            def b_shift(u, j):
                ve.wait_ge(S("b_scores"), u + 1 + 4)
                sc = ps[:, 2 * j:2 * j + 2, :].rearrange("p a (h n) -> p (a h) n", h=4)
                nc.vector.tensor_reduce(mxb[:, j, :], sc, AX, ALU.max).then_inc(S("b_max"), 1)
                ve.wait_ge(S("b_max"), u + 1)
                if not (isinstance(u, int) and u < 2):
                    ve.wait_ge(S("b_pturned"), u - 1)
                nc.vector.tensor_tensor(PB[j], sc, mxb[:, j, :].unsqueeze(2).broadcast_to([P, HH, P]), ALU.subtract)\
                  .then_inc(S("b_shifted"), 1)

            def b_output(u, tile, j):
                ve.wait_ge(S("b_pv"), u + 1 + 4)
                nc.vector.tensor_copy(OTb[:, 2 * j:2 * j + 2, bass.ds(P * tile, P)],
                                      ps[:, 4 + 2 * j, 0:2 * P].rearrange("p (q n) -> p q n", q=2)).then_inc(S("b_out"), 1)

            def b_vector(i, first=False, last=False):
                for k in range(4):
                    u, j = 4 * i + k, k % 2
                    if not (last and k >= 2):
                        b_shift(u + 2, j)
                    if not (first and k == 0):
                        b_output(u - 1, 2 * i + (k - 1) // 2, 1 - j)

            b_shift(0, 0)
            b_shift(1, 1)
            b_vector(0, first=True)
            with ve.Fori(1, BU // 4 - 1) as i:
                b_vector(i)
            b_vector(BU // 4 - 1, last=True)
            b_output(BU - 1, NT - 1, 1)
            head_norm_vector(ve, 1)
            ve.wait_ge(S("xn_biased"), 1)
            for q in range(NQ):
                ve.wait_ge(S("head_proj"), NQ + q + 1)
                xq = XN[:, 4 * q:4 * q + 4, :].rearrange("p t c -> p (t c)")
                nc.vector.tensor_tensor(xq, xq, ps[:, 6 + q % 2, :], ALU.add).then_inc(S("xb1"), 1)
            norm_vector(ve, "nb2", XN, HN, S("xb1"))
            turn_vector(ve, "b2", XT, colb[:, LN2G:LN2G + 1], colb[:, LN2B:LN2B + 1])
            ve.wait_ge(S("x_plus"), 1)
            for s in range(NQ):
                ve.wait_ge(S("mlp_down"), s + 1)
                xq = X[:, 4 * s:4 * s + 4, :].rearrange("p t c -> p (t c)")
                nc.vector.tensor_tensor(xq, xq, ps[:, 4 + s % 2, :], ALU.add).then_inc(S("x3"), 1)
            norm_vector(ve, "n1", X, XN, S("x3"))
            expert_in_vector(ve, "m1")
            route_vector(ve, "m1")
            comb_vector(ve, "m1")
            experts_vector(ve, "m1", 1)

        @block.tensor
        def _(pe):
            pe.nop().then_inc(S("pv_done"), 2)
            pe.nop().then_inc(S("down_done"), 8)
            pe.wait_ge(S("consts_in"), 16 * 18)
            turn_tensor(pe, "na", XN, S("na_normed"))
            qk_tensor(pe, "a", wqkva, "na")
            v_tensor(pe, "a", wqkva)

            def max_item(i, b, k):
                c = B * i + b
                item = ITEM_LIST[k]
                first = isinstance(c, int) and c == 0
                if not (first and k < 2):
                    pe.wait_ge(S("max_done"), ITEMS * c + k - 1)
                if item[0] == "max":
                    _, nh, h, nt = item
                    n0 = 512 * nh + P * nt
                    for mh in range(2):
                        last = nc.tensor.matmul(ps[:, MB[k % 2] + mh, :], QZ[b][0:96, h // 2, h % 2, n0:n0 + P],
                                                KA[b][0:96, h // 2, 512 * mh:512 * mh + 512], start=True, stop=True)
                    last.then_inc(S("max_full"), 1)
                else:
                    nh = item[1]
                    pe.wait_ge(S("max_done"), ITEMS * c + LAST_MAX[nh] + 1)
                    nc.tensor.transpose(ps[0:16, MB[k % 2], 0:P], mx[nh][:, :], ident[:, :]).then_inc(S("max_full"), 1)

            def weigh(i, b, u):
                nh, mt = u // MT, u % MT
                pe.wait_ge(S("exp_done"), 64 + 128 * i + 64 * b + 4 * u + 4)
                if mt == 0:
                    if u == 0:
                        pe.wait_ge(S("vs_in"), 2 * i + b + 1)
                    pe.wait_ge(S("o_out"), 4 * i + 2 * b + nh + 1)
                for h in range(HQ):
                    last = nc.tensor.matmul(ps[32 * h:32 * h + 32, OB, :], Vs[b][:, mt, h, :], EX[u % 2][:, h, :],
                                            start=(mt == 0), stop=(mt == MT - 1))
                last.then_inc(S("pv_done"), 1)

            def scores(i, b, u, more):
                nh, mt = u // MT, u % MT
                if u < 6:
                    at = ITEMS - CARRY + sum(PLAN[:u])
                    todo = [(i, b, k) for k in range(at, at + PLAN[u])]
                else:
                    at = sum(PLAN[6:u])
                    todo = [(i + b, 1 - b, k) for k in range(at, at + PLAN[u])] if more else []
                if mt == 0:
                    pe.wait_ge(S(f"mrow_in{b}{nh}"), 16 * i + 16)
                if u == 6 and more:
                    pe.wait_ge(S(f"kq_in{1 - b}"), 64 * (i + b) + 64)
                for h in range(HQ):
                    k = 4 * u + h
                    back = 3 if k >= 3 else {0: 1, 1: 4, 2: 4}[k]
                    pe.wait_ge(S("exp_done"), 64 + 128 * i + 64 * b + k - back + 1)
                    nc.tensor.matmul(ps[:, SB[k % 3], :], KA[b][0:99, h // 2, mt * P:(mt + 1) * P],
                                     QZ[b][0:99, h // 2, h % 2, 512 * nh:512 * nh + 512],
                                     start=True, stop=True).then_inc(S("s_full"), 1)
                    if todo and h < 3:
                        max_item(*todo.pop(0))

            def combination(i, b, more):
                for u in range(1, UNITS):
                    scores(i, b, u, more)
                    weigh(i, b, u - 1)
                if more:
                    scores(i + b, 1 - b, 0, True)
                weigh(i, b, UNITS - 1)

            pe.nop().then_inc(S("o_out"), 1)
            pe.wait_ge(S("kq_in0"), 64)
            pe.wait_ge(S("a_v_out"), NQ)
            pe.wait_ge(S("a_k_out"), NQ)
            for k in range(ITEMS - CARRY):
                max_item(0, 0, k)
            scores(0, 0, 0, True)
            with pe.Fori(0, QUADS - 1) as i:
                combination(i, 0, True)
                combination(i, 1, True)
            combination(QUADS - 1, 0, True)
            combination(QUADS - 1, 1, False)

            pe.wait_ge(S("o_out"), 1 + 4 * QUADS)
            head_project_tensor(pe, 0, OT, wpa, S("x1"))
            route_tensor(pe, "m0", XN, S("n0_normed"))
            experts_tensor(pe, "m0", 0)
            turn_tensor(pe, "b1", HN, S("nb1_normed"))
            qk_tensor(pe, "b", wqkvb, "b1")
            v_tensor(pe, "b", wqkvb)
            pe.wait_ge(S("b_v_out"), NQ)
            pe.wait_ge(S("b_k_out"), NQ)
            pe.nop().then_inc(S("b_scores"), 4)
            pe.nop().then_inc(S("b_pv"), 4)
            pe.nop().then_inc(S("b_out"), 2)

            def b_scores(u, tile, half, j):
                if not (isinstance(u, int) and u < 2):
                    pe.wait_ge(S("b_shifted"), u - 1)
                for bank in (2 * j, 2 * j + 1):
                    nc.tensor.matmul(ps[:, bank, :].rearrange("p (h n) -> p h n", h=4)[:, :, BK:P], identb[:, :],
                                     causal[:, BK:P].unsqueeze(1).broadcast_to([P, 4, BK]), start=True, stop=True,
                                     skip_group_check=True)
                    for hh in range(4):
                        h = HH * half + 4 * (bank - 2 * j) + hh
                        for w in range(2):
                            last = nc.tensor.matmul(ps[BK * w:BK * w + BK, bank, hh * P:(hh + 1) * P],
                                                    QB[tile][0:KR, h, BK * w:BK * w + BK],
                                                    KB[tile][0:KR, h, BK * w:BK * w + P],
                                                    start=False, stop=True, skip_group_check=True)
                last.then_inc(S("b_scores"), 1)

            def b_values(u, k, i):
                j, tile, half = k % 2, k // 2, k % 2
                pe.wait_ge(S("b_pt"), u + 1)
                if half == 0:
                    pe.wait_ge(S(f"b_v_in{tile}"), i + 1)
                for hh in range(HH):
                    for w in range(2):
                        n0 = P * (hh // 4) + BK * w
                        ins = nc.tensor.matmul(ps[32 * (hh % 4):32 * (hh % 4) + 32, 4 + 2 * j, n0:n0 + BK],
                                               VWs[tile][:, w, HH * half + hh, :], PT[j][:, hh, BK * w:BK * w + BK],
                                               start=True, stop=True, skip_group_check=True)
                ins.then_inc(S("b_pv"), 1)

            def b_tensor(i, first=False, last=False):
                for k in range(4):
                    u, j, tile, half = 4 * i + k, k % 2, k // 2, k % 2
                    if not (last and k >= 2):
                        if half == 0:
                            pe.wait_ge(S(f"b_qk_in{1 - tile}"), 32 * i + 32 + 32 * tile)
                        b_scores(u + 2, 1 - tile, half, j)
                    pe.wait_ge(S("b_exp"), u + 1)
                    pe.wait_ge(S("b_out"), u + 1)
                    for hh in range(HH):
                        ins = nc.tensor.transpose(ps[:, 4 + 2 * j + hh // 4, (hh % 4) * P:(hh % 4 + 1) * P],
                                                  PB[j][:, hh, :], ident[:, :])
                    ins.then_inc(S("b_pturned"), 1)
                    if not (first and k == 0):
                        b_values(u - 1, (k - 1) % 4, i)

            pe.wait_ge(S("b_qk_in0"), 32)
            b_scores(0, 0, 0, 0)
            b_scores(1, 0, 1, 1)
            b_tensor(0, first=True)
            with pe.Fori(1, BU // 4 - 1) as i:
                b_tensor(i)
            b_tensor(BU // 4 - 1, last=True)
            b_values(BU - 1, 3, BU // 4 - 1)
            pe.wait_ge(S("b_out"), 2 + BU)
            head_project_tensor(pe, 1, OTb, wob, S("xb1"))
            turn_tensor(pe, "b2", HN, S("nb2_normed"))
            for q in range(NQ):
                turned_wait(pe, "b2", q)

            def mlp_down(s):
                pe.wait_ge(S("mlp_gelu"), 4 * s + 4)
                if s >= 2:
                    pe.wait_ge(S("x3"), s - 1)
                else:
                    pe.wait_ge(S("xb1"), NQ)
                for j in range(4):
                    for f in range(FC):
                        last = nc.tensor.matmul(ps[:, 4 + s % 2, j * P:(j + 1) * P], Gb[s % 2][:, f, j * P:(j + 1) * P],
                                                w2b[:, f, :], start=(f == 0), stop=(f == FC - 1))
                last.then_inc(S("mlp_down"), 1)

            for s in range(NQ):
                for f in range(FC):
                    if s:
                        pe.wait_ge(S("mlp_gelu"), 4 * s - 3 + f)
                    nc.tensor.matmul(ps[:, f, :], w1b[:, f * P:(f + 1) * P], XT[:, s * QW:(s + 1) * QW],
                                     start=True, stop=True).then_inc(S("mlp_up"), 1)
                if s:
                    mlp_down(s - 1)
            mlp_down(NQ - 1)
            route_tensor(pe, "m1", XN, S("n1_normed"))
            experts_tensor(pe, "m1", 1)


def kernel(**inputs):
    import numpy as np
    import concourse.bacc as bacc
    from concourse.bass_utils import run_bass_kernel_spmd

    a = {k: np.ascontiguousarray(v) for k, v in inputs.items()}
    import ml_dtypes
    f32 = np.float32

    def blockdiag(w):
        g, ci, co = w.shape
        full = np.zeros((g * ci, g * co), f32)
        for k in range(g):
            full[k * ci:(k + 1) * ci, k * co:(k + 1) * co] = w[k]
        return full

    def rows(v):
        return np.ascontiguousarray(np.broadcast_to(v, (P, v.shape[0])))

    bq = a["L0_attn_b_b_qkv"]
    cols = [a["L0_attn_b_ln1_g"], a["L0_attn_b_ln1_b"], a["L0_attn_b_ln2_g"], a["L0_attn_b_ln2_b"],
            bq[0:P], bq[P:2 * P]] + [a["L0_attn_b_b1"][f * P:(f + 1) * P] for f in range(FC)]
    cols += [np.zeros(P, f32)] * (12 - len(cols))
    causal = np.zeros((P, P), f32)
    for i in range(P):
        causal[i, BK + i % BK + 1:] = -1e30
    arrays = {
        "x": a["L0_attn_a_x"],
        "wqkva": blockdiag(a["L0_attn_a_w_qkv"]), "wpa": blockdiag(a["L0_attn_a_w_proj"]), "bpa": rows(a["L0_attn_a_b_proj"]),
        "ident": np.eye(P, dtype=f32), "identb": np.eye(P, dtype=ml_dtypes.bfloat16),
        "causal": causal.astype(ml_dtypes.bfloat16),
        "tri": np.ascontiguousarray(np.broadcast_to(np.tril(np.ones((E, E), ml_dtypes.bfloat16), -1), (P, E, E))),
        "wqkvb": a["L0_attn_b_w_qkv"], "colb": np.ascontiguousarray(np.stack(cols, axis=1)),
        "bvb": rows(bq[2 * P:3 * P]), "bob": rows(a["L0_attn_b_b_out"]), "b2b": rows(a["L0_attn_b_b2"]),
        "wob": a["L0_attn_b_w_out"], "w1b": a["L0_attn_b_w1"],
        "w2b": np.ascontiguousarray(a["L0_attn_b_w2"].reshape(FC, P, P).transpose(1, 0, 2)),
        "rw": np.ascontiguousarray(a["L0_ffn_router_w"].T),
        "b1e": np.ascontiguousarray(a["L0_ffn_b1"].reshape(E, FC, P).transpose(2, 0, 1)),
        "b2e": a["L0_ffn_b2"],
        "ffn_w1": np.ascontiguousarray(a["L0_ffn_w1"].transpose(0, 2, 1)),
        "ffn_w2": np.ascontiguousarray(a["L0_ffn_w2"].reshape(E, P, FC, P).transpose(0, 3, 2, 1)).reshape(E, P, FF),
    }
    nc = bacc.Bacc("TRN2", target_bir_lowering=False, num_devices=1)
    dram = {k: nc.dram_tensor(f"in_{k}", v.shape, mybir.dt.from_np(v.dtype), kind="ExternalInput").ap()
            for k, v in arrays.items()}
    out = nc.dram_tensor("out", (B, N, P), F32, kind="ExternalOutput").ap()
    build(nc, dram, out)
    r = run_bass_kernel_spmd(nc, [{f"in_{k}": v for k, v in arrays.items()}], core_ids=[0])
    return r.results[0]["out"]
```

```python
from contextlib import ExitStack

import concourse.bass as bass
from concourse import mybir

F32 = mybir.dt.float32
F32R = mybir.dt.float32r
BF16 = mybir.dt.bfloat16
ALU = mybir.AluOpType
ACT = mybir.ActivationFunctionType
AX = mybir.AxisListType.X

P = 128
B = 2
N = 1024
T = B * N
NT = T // P
NQ = 4
QW = T // NQ
H = 16
D = P // H
HQ = 4
QUADS = H // HQ
SCALE = float(D) ** -0.5
EPS = 1e-5
K_PARTS = (0, 0, 0, 1, 1, 2)
Q_PARTS = (0, 1, 2, 0, 1, 0)
NR = len(K_PARTS)
KR = NR * D
MT = N // P
UNITS = 2 * MT
ITEMS = 34
E = 8
FF = 512
FC = FF // P
BK = 64
KW = 3 * BK
HH = H // 2
BU = 2 * NT
PADN = N + BK
VW = D + 1
PLAN = (3, 2, 2, 2, 2, 2, 2, 2, 2, 2, 2, 2, 2, 2, 2, 3)
NEXT = 4
CARRY = sum(PLAN[:NEXT])
assert sum(PLAN) == ITEMS


def max_items():
    halves = [[("max", nh, h, nt) for nt in range(4) for h in range(HQ)] for nh in range(2)]
    return halves[0] + halves[1][:1] + [("turn", 0)] + halves[1][1:] + [("turn", 1)]


ITEM_LIST = max_items()
assert len(ITEM_LIST) == ITEMS


def slot_item(k, first, last):
    if k == 0 and not first:
        return ITEM_LIST[-1], -1
    if k == ITEMS - 1 and not last:
        return ITEM_LIST[0], 1
    return ITEM_LIST[k], 0


def turned_at(nh, last):
    return 18 if nh == 0 else ITEMS if last else ITEMS + 1


def build(nc, dram, out):
    with ExitStack() as ctx:
        def sb(name, shape, dt=F32):
            return ctx.enter_context(nc.sbuf_tensor(name, shape, dt))

        def scratch(name, shape, dt):
            return nc.dram_tensor(name, shape, dt, kind="Internal").ap()

        sems = {}

        def S(name):
            if name not in sems:
                sems[name] = ctx.enter_context(nc.semaphore(name))
            return sems[name]

        X = sb("X", [P, NT, P])
        XN = sb("XN", [P, NT, P])
        HN = sb("HN", [P, NT, P])
        XT = sb("XT", [P, T])
        st = sb("st", [P, NT, 6])
        mv = sb("mv", [P, NT, 2])
        rstd = sb("rstd", [P, NT])
        mhalf = sb("mhalf", [P, NT])
        ident = sb("ident", [P, P])
        identb = sb("identb", [P, P], BF16)
        causal = sb("causal", [P, P], BF16)
        wqkva = sb("wqkva", [P, 3 * P])
        wpa = sb("wpa", [P, P])
        rsa = sb("rsa", [P, NT, H])
        warm = sb("warm", [P, 1])
        bpa = sb("bpa", [P, P])
        wqkvb = sb("wqkvb", [P, 3 * P])
        colb = sb("colb", [P, 12])
        bvb = sb("bvb", [P, P])
        bob = sb("bob", [P, P])
        b2b = sb("b2b", [P, P])
        wob = sb("wob", [P, P])
        w1b = sb("w1b", [P, FF])
        w2b = sb("w2b", [P, FC, P])
        rw = sb("rw", [P, E])
        b1e = sb("b1e", [P, E, FC])
        b1s = sb("b1s", [P, 2, FC])
        b2e = sb("b2e", [E, P])
        tri = sb("tri", [P, E, E], BF16)
        L = sb("L", [P, NT, E])
        beats = sb("beats", [P, NT, E, E], BF16)
        ties = sb("ties", [P, NT, E, E], BF16)
        rank = sb("rank", [P, NT, E])
        lmax = sb("lmax", [P, NT])
        comb = sb("comb", [P, NT, E])
        zer = sb("zer", [P, BK], BF16)

        with ExitStack() as phase:
            def pb(name, shape, dt=F32):
                return phase.enter_context(nc.sbuf_tensor(name, shape, dt))

            QF = pb("QF", [P, T])
            KF = pb("KF", [P, T])
            parts = pb("parts", [P, 3, T], BF16)
            KA = [pb(f"KA{b}", [P, 2, N], BF16) for b in range(B)]
            QZ = [pb(f"QZ{b}", [P, 2, 2, N], BF16) for b in range(B)]
            EX = [pb(f"EX{j}", [P, HQ, 512]) for j in range(2)]
            OT = pb("OT", [P, QUADS, T])
            Vn = pb("Vn", [P, QUADS * B, MT, HQ * D])
            Vs = [pb(f"Vs{b}", [P, MT, HQ, 32]) for b in range(B)]
            mx = [pb(f"mx{j}", [P, 16]) for j in range(2)]
            neg = [pb(f"neg{j}", [16, P]) for j in range(2)]
            nres = pb("nres", [16, P])
            mparts = [pb(f"mparts{j}", [16, 3, P], BF16) for j in range(2)]
            partk = pb("partk", [P, 3, T], BF16)
        with ExitStack() as phase:
            def pb(name, shape, dt=F32):
                return phase.enter_context(nc.sbuf_tensor(name, shape, dt))

            XH = pb("XH", [P, T], F32R)
            XL = pb("XL", [P, T], F32R)
            CB = [pb(f"CB{j}", [P, T]) for j in range(2)]
            WR = [pb(f"WR{j}", [P, 2, FF]) for j in range(2)]
            WH = [pb(f"WH{j}", [P, 2, FF], F32R) for j in range(2)]
            WL = [pb(f"WL{j}", [P, 2, FF], F32R) for j in range(2)]
            G = [pb(f"G{j}", [P, FC, 512]) for j in range(2)]
            GH = [pb(f"GH{j}", [P, FC, 512], F32R) for j in range(2)]
            GL = [pb(f"GL{j}", [P, FC, 512], F32R) for j in range(2)]
            combT = pb("combT", [E, T])
        with ExitStack() as phase:
            def pb(name, shape, dt=F32):
                return phase.enter_context(nc.sbuf_tensor(name, shape, dt))

            partsb = pb("partsb", [P, 3, T], BF16)
            partkb = pb("partkb", [P, 3, T], BF16)
            V9 = pb("V9", [P, 2, NT, H, VW])
            QB = [pb(f"QB{j}", [P, H, P], BF16) for j in range(2)]
            KB = [pb(f"KB{j}", [P, H, KW], BF16) for j in range(2)]
            VWs = [pb(f"VWs{j}", [P, 2, H, 32]) for j in range(2)]
            PB = [pb(f"PB{j}", [P, HH, P])[:, :, :] for j in range(2)]
            PT = [pb(f"PT{j}", [P, HH, P])[:, :, :] for j in range(2)]
            mxb = pb("mxb", [P, 2, HH])
            Gb = [pb(f"Gb{j}", [P, FC, 512]) for j in range(2)]
            with ExitStack() as early:
                QFb = early.enter_context(nc.sbuf_tensor("QFb", [P, T], F32))
                KFb = early.enter_context(nc.sbuf_tensor("KFb", [P, T], F32))
            OTb = pb("OTb", [P, QUADS, T])

        ps = ctx.enter_context(nc.psum_tensor("ps", [P, 8, 512], F32))
        SB, OB, MB = (0, 1, 2), 3, (4, 6)

        kst = scratch("kst", (H, KR, T), BF16)
        qst = scratch("qst", (H, KR, T), BF16)
        mrow = scratch("mrow", (B, 2, 3, 16, P), BF16)
        kstb = scratch("kstb", (H, KR, B * PADN), BF16)
        qstb = scratch("qstb", (H, KR, T), BF16)
        cst = scratch("cst", (E, T), F32)

        kst_q = kst.rearrange("(q a j) r t -> q j r a t", a=2, j=2)
        qst_q = qst.rearrange("(q a j) r t -> q j r a t", a=2, j=2)

        LN1G, LN1B, LN2G, LN2B, BQ, BKC, B1C = 0, 1, 2, 3, 4, 5, 6

        block = ctx.enter_context(nc.Block())

        def hold(eng, sem, value):
            eng.wait_ge(sem, value)
            eng.nop(nofuse=True)

        NORMS = ("na", "n0", "nb", "nb1", "nb2", "n1")

        def norm_moments(ve, tag, src, q):
            k = NQ * NORMS.index(tag)
            for t in range(4 * q, 4 * q + 4):
                ins = nc.vector.bn_stats(st[:, t, :], src[:, t, :])
            ins.then_inc(S("norm_stats"), 1)
            ve.wait_ge(S("norm_stats"), k + q + 1)
            for t in range(4 * q, 4 * q + 4):
                ins = nc.vector.bn_aggr(mv[:, t, :], st[:, t, :])
            ins.then_inc(S("norm_moments"), 1)

        def norm_apply(ve, tag, src, dst):
            k = NQ * NORMS.index(tag)
            for t in range(NT):
                if t % 4 == 0:
                    ve.wait_ge(S("norm_rstd"), k + t // 4 + 1)
                nc.vector.tensor_scalar(dst[:, t, :], src[:, t, :], mv[:, t, 0:1], rstd[:, t:t + 1],
                                        ALU.subtract, ALU.mult).then_inc(S(f"{tag}_normed"), 1)

        def norm_vector(ve, tag, src, dst, ready=None):
            for q in range(NQ):
                if ready is not None:
                    ve.wait_ge(*ready(q))
                norm_moments(ve, tag, src, q)
            norm_apply(ve, tag, src, dst)

        def norm_gpsimd(g, tag):
            k = NQ * NORMS.index(tag)
            for q in range(NQ):
                c = slice(4 * q, 4 * q + 4)
                g.wait_ge(S("norm_moments"), k + q + 1)
                nc.gpsimd.tensor_scalar(rstd[:, c], mv[:, c, 1], EPS, None, ALU.add).then_inc(S("norm_guarded"), 1)
                g.wait_ge(S("norm_guarded"), k + q + 1)
                nc.gpsimd.tensor_tensor(rstd[:, c], rstd[:, c], mhalf[:, c], ALU.pow).then_inc(S("norm_rstd"), 1)

        def turn_tensor(pe, tag, src, ready):
            for q in range(NQ):
                pe.wait_ge(ready, 4 * q + 4)
                for j in range(4):
                    last = nc.tensor.transpose(ps[:, q, j * P:(j + 1) * P], src[:, 4 * q + j, :], ident[:, :])
                last.then_inc(S(f"{tag}_turned"), 1)

        def turn_scalar(act, tag, dst, gain=None, shift=None):
            for q in (0, 2):
                act.wait_ge(S(f"{tag}_turned"), q + 1)
                d = dst[:, q * QW:(q + 1) * QW]
                if gain is None:
                    nc.scalar.activation(d, ps[:, q, :], ACT.Copy).then_inc(S(f"{tag}_even"), 1)
                else:
                    nc.scalar.activation(d, ps[:, q, :], ACT.Identity, bias=shift, scale=gain).then_inc(S(f"{tag}_even"), 1)

        def turn_vector(ve, tag, dst, gain=None, shift=None):
            for q in (1, 3):
                ve.wait_ge(S(f"{tag}_turned"), q + 1)
                d = dst[:, q * QW:(q + 1) * QW]
                if gain is None:
                    nc.vector.tensor_copy(d, ps[:, q, :]).then_inc(S(f"{tag}_odd"), 1)
                else:
                    nc.vector.tensor_scalar(d, ps[:, q, :], gain, shift, ALU.mult, ALU.add).then_inc(S(f"{tag}_odd"), 1)

        def turned_wait(eng, tag, q):
            eng.wait_ge(S(f"{tag}_odd" if q % 2 else f"{tag}_even"), q // 2 + 1)

        def split_vector(ve, tag, src, parts, b):
            c = slice(b * N, (b + 1) * N)
            done = S(f"{tag}_split")
            res = HN[:, :, :].rearrange("p t c -> p (t c)")
            ve.wait_ge(S(f"{tag}_hi"), 2 * b + 2)
            nc.vector.tensor_tensor(res[:, c], src[:, c], parts[:, 0, c], ALU.subtract).then_inc(done, 1)
            ve.wait_ge(done, 3 * b + 1)
            nc.vector.tensor_copy(parts[:, 1, c], res[:, c]).then_inc(done, 1)
            ve.wait_ge(done, 3 * b + 2)
            nc.vector.tensor_tensor(parts[:, 2, c], res[:, c], parts[:, 1, c], ALU.subtract).then_inc(done, 1)
            ve.wait_ge(done, 3 * b + 3)

        def stacks_sync(sp, tag, b, qparts, qdst, kparts, kdst, kat, first=0, end=6):
            def rows(which, parts, dst, order, part, at):
                if part == 0:
                    sp.wait_ge(S(f"{tag}{which}_hi"), 2 * b + 2)
                else:
                    sp.wait_ge(S(f"{tag}{which}_split"), 3 * b + 1 + part)
                for r in range(NR):
                    if order[r] == part:
                        sp.dma_start(dst.rearrange("h (r d) t -> r h d t", r=NR)[r, :, :, at:at + N],
                                     parts[:, part, b * N:(b + 1) * N]).then_inc(S(f"{tag}{which}_stacked{b}"), 16)

            q = ("q", qparts, qdst, Q_PARTS)
            k = ("k", kparts, kdst, K_PARTS)
            for who, part in ((q, 0), (k, 0), (q, 1), (q, 2), (k, 1), (k, 2))[first:end]:
                rows(*who, part, kat if who is k else b * N)

        def qk_tensor(pe, tag, w, turned):
            for q in range(NQ):
                turned_wait(pe, turned, q)
                for which in range(2):
                    nc.tensor.matmul(ps[:, 4 * which + q, :], w[:, which * P:(which + 1) * P],
                                     XT[:, q * QW:(q + 1) * QW], start=True, stop=True).then_inc(S(f"{tag}_qk"), 1)

        def v_tensor(pe, tag, w):
            for q in range(NQ):
                pe.wait_ge(S(f"{tag}_q_out"), q + 1)
                for j in range(4):
                    t = 4 * q + j
                    last = nc.tensor.matmul(ps[:, q, j * P:(j + 1) * P], XT[:, t * P:(t + 1) * P], w[:, 2 * P:3 * P],
                                            start=True, stop=True)
                last.then_inc(S(f"{tag}_v"), 1)

        def head_turn(pe, src, t, bank):
            for quad in range(QUADS):
                ins = nc.tensor.transpose(ps[:, bank, quad * P:(quad + 1) * P], src[:, quad, t * P:(t + 1) * P], ident[:, :])
            ins.then_inc(S("o_turned"), 1)

        def head_norm(ve, r, t, bank):
            ve.wait_ge(S("o_turned"), NT * r + t + 1)
            o = ps[:, bank, :].rearrange("p (h c) -> p h c", h=H)
            nc.vector.reciprocal(rsa[:, t, :], o[:, :, D]).then_inc(S("rs_ready"), 1)
            ve.wait_ge(S("rs_ready"), NT * r + t + 1)
            nc.vector.tensor_tensor(HN[:, t, :].rearrange("p (h d) -> p h d", h=H), o[:, :, 0:D],
                                    rsa[:, t, :].unsqueeze(2).broadcast_to([P, H, D]), ALU.mult)\
              .then_inc(S("o_normed"), 1)

        def head_turn_back(pe, r, q, bank, behind):
            pe.wait_ge(S("o_normed"), NT * r + 4 * q + 4)
            if q >= behind:
                pe.wait_ge(S("head_xt"), NQ * r + q + 1 - behind)
            for j in range(4):
                ins = nc.tensor.transpose(ps[:, bank, j * P:(j + 1) * P], HN[:, 4 * q + j, :], ident[:, :])
            ins.then_inc(S("head_back"), 1)

        def head_project(pe, r, q, w, bank, before=None):
            pe.wait_ge(S("head_xt"), NQ * r + q + 1)
            if before is not None:
                pe.wait_ge(*before)
            for j in range(4):
                t = 4 * q + j
                ins = nc.tensor.matmul(ps[:, bank, j * P:(j + 1) * P], XT[:, t * P:(t + 1) * P], w[:, :],
                                       start=True, stop=True)
            ins.then_inc(S("head_proj"), 1)

        def head_norm_vector(ve, r, first=0):
            for t in range(first, NT):
                head_norm(ve, r, t, t % 4)

        def head_back_scalar(act, r, first=0):
            for q in range(first, NQ):
                act.wait_ge(S("head_back"), NQ * r + q + 1)
                nc.scalar.activation(XT[:, q * QW:(q + 1) * QW], ps[:, 4 + q % 2, :], ACT.Copy).then_inc(S("head_xt"), 1)

        def head_project_tensor(pe, r, src, w, added, first=0):
            for s in range(first, NQ + 2):
                if s < NQ:
                    for t in range(4 * s, 4 * s + 4):
                        if t >= 4 * first + 4:
                            pe.wait_ge(S("o_normed"), NT * r + t - 3)
                        head_turn(pe, src, t, t % 4)
                if first + 1 <= s <= NQ:
                    head_turn_back(pe, r, s - 1, 4 + (s - 1) % 2, 2)
                if s >= first + 2:
                    q = s - 2
                    head_project(pe, r, q, w, 6 + q % 2, (added, q - 1) if q >= 2 else None)

        ROUTED = ((0, 4), (4, NT))

        def expert_in_scalar(act, m):
            nc.scalar.activation(warm[:, :], mhalf[:, 0:1], ACT.Exp)
            for q in range(NQ):
                act.wait_ge(S(f"{m}_turned"), q + 1)
                c = slice(q * QW, (q + 1) * QW)
                nc.scalar.activation(XT[:, c], ps[:, q, :], ACT.Copy).then_inc(S(f"{m}_xt"), 1)
                nc.scalar.activation(XH[:, c], ps[:, q, :], ACT.Copy).then_inc(S(f"{m}_xh"), 1)

        def expert_in_vector(ve, m, q):
            c = slice(q * QW, (q + 1) * QW)
            ve.wait_ge(S(f"{m}_xh"), q + 1)
            nc.vector.tensor_tensor(XL[:, c], XT[:, c], XH[:, c], ALU.subtract).then_inc(S(f"{m}_xl"), 1)

        def route_tensor(pe, m, src, normed):
            for q in range(NQ + 1):
                if q < NQ:
                    pe.wait_ge(normed, 4 * q + 4)
                    for j in range(4):
                        last = nc.tensor.transpose(ps[:, q, j * P:(j + 1) * P], src[:, 4 * q + j, :], ident[:, :])
                    last.then_inc(S(f"{m}_turned"), 1)
                if q:
                    pe.wait_ge(S(f"{m}_xt"), q)
                    for t in range(4 * q - 4, 4 * q):
                        last = nc.tensor.matmul(ps[:, 6 if q == 1 else 7, t * E:(t + 1) * E], XT[:, t * P:(t + 1) * P], rw[:, :],
                                                start=True, stop=True)
                    if q in (1, NQ):
                        last.then_inc(S(f"{m}_logits"), 1)

        ROUTE_STEPS, SHIFTED = 12, 8

        def route_vector(ve, m):
            done = S(f"{m}_route")
            n = [0]

            def step(ins):
                n[0] += 1
                ins.then_inc(done, 1)
                ve.wait_ge(done, n[0])

            for part, (t0, t1) in enumerate(ROUTED):
                nt = t1 - t0
                l, r, c, lm = L[:, t0:t1, :], rank[:, t0:t1, :], comb[:, t0:t1, :], lmax[:, t0:t1]
                tie, beat = ties[:, t0:t1, :, :], beats[:, t0:t1, :, :]
                ve.wait_ge(S(f"{m}_logits"), part + 1)
                step(nc.vector.tensor_copy(l.rearrange("p t e -> p (t e)"), ps[:, 6 + part, t0 * E:t1 * E]))
                mine = l.unsqueeze(3).broadcast_to([P, nt, E, E])
                theirs = l.unsqueeze(2).broadcast_to([P, nt, E, E])
                step(nc.vector.tensor_tensor(tie, theirs, mine, ALU.is_equal))
                step(nc.vector.tensor_tensor(tie, tie, tri[:, :, :].unsqueeze(1).broadcast_to([P, nt, E, E]), ALU.mult))
                step(nc.vector.tensor_tensor(beat, theirs, mine, ALU.is_gt))
                step(nc.vector.tensor_tensor(beat, beat, tie, ALU.add))
                step(nc.vector.tensor_reduce(r, beat, AX, ALU.add))
                step(nc.vector.tensor_reduce(lm, l, AX, ALU.max))
                step(nc.vector.tensor_tensor(l, l, lm.unsqueeze(2).broadcast_to([P, nt, E]), ALU.subtract))
                for q in ((0,), (2, 3))[part]:
                    expert_in_vector(ve, m, q)
                step(nc.vector.tensor_scalar(r, r, 2.0, None, ALU.is_lt))
                ve.wait_ge(S(f"{m}_exps"), part + 1)
                step(nc.vector.tensor_tensor(c, c, r, ALU.mult))
                step(nc.vector.tensor_reduce(lm, c, AX, ALU.add))
                step(nc.vector.reciprocal(lm, lm))
                nc.vector.tensor_tensor(c, c, lm.unsqueeze(2).broadcast_to([P, nt, E]), ALU.mult)\
                  .then_inc(S(f"{m}_comb"), 1)
                if part == 0:
                    expert_in_vector(ve, m, 1)

        def route_scalar(act, m, part):
            t0, t1 = ROUTED[part]
            act.wait_ge(S(f"{m}_route"), ROUTE_STEPS * part + SHIFTED)
            nc.scalar.activation(comb[:, t0:t1, :], L[:, t0:t1, :], ACT.Exp).then_inc(S(f"{m}_exps"), 1)

        def comb_tensor(pe, m, part):
            pe.wait_ge(S(f"{m}_comb"), part + 1)
            for t in range(*ROUTED[part]):
                last = nc.tensor.transpose(ps[0:E, 4 + t // 4, (t % 4) * P:(t % 4 + 1) * P], comb[:, t, :], ident[:, :])
            last.then_inc(S(f"{m}_combT"), 1)

        def comb_scalar(act, m, part):
            t0, t1 = ROUTED[part]
            act.wait_ge(S(f"{m}_combT"), part + 1)
            nc.scalar.activation(combT[:, t0 * P:t1 * P],
                                 ps[0:E, 4 + t0 // 4:4 + t1 // 4, :].rearrange("p a n -> p (a n)"), ACT.Copy)\
              .then_inc(S(f"{m}_combT_out"), 1)

        def comb_bias(pe, m):
            for q in range(NQ):
                pe.wait_ge(S(f"{m}_combT_out"), 1 if q == 0 else 2)
                nc.tensor.matmul(ps[:, 4 + q, :], b2e[:, :], combT[:, q * QW:(q + 1) * QW], start=True, stop=False)

        def up(i, s, chunks=range(FC)):
            p, q = s // 4 % 2, s % 4
            for f in chunks:
                w = slice(f * P, (f + 1) * P)
                nc.tensor.wait_ge(S("gelu_out"), 32 * i + 4 * s + f + 1)
                for n, (a, x) in enumerate(((WH, XH), (WH, XL), (WL, XH))):
                    ins = nc.tensor.matmul(ps[:, f, :], a[p][:, 0, w], x[:, q * QW:(q + 1) * QW],
                                           start=(n == 0), stop=(n == 2))
                ins.then_inc(S("up_done"), 1)

        def down(i, s, last):
            p, q = s // 4, s % 4
            for f in range(FC):
                if f % 2 == 0:
                    nc.tensor.wait_ge(S("halved"), 4 + 16 * i + 2 * s + f // 2 + 1)
                w = slice(f * P, (f + 1) * P)
                for n, (a, g) in enumerate(((WH, GH), (WH, GL), (WL, GH))):
                    ins = nc.tensor.matmul(ps[:, 4 + q, :], a[p][:, 1, w], g[s % 2][:, f, :], start=False,
                                           stop=(last and s >= 4 and f == FC - 1 and n == 2))
            ins.then_inc(S("down_done"), 1)

        def experts_tensor(pe, m, r):
            def body(i, last):
                for s in range(8):
                    if not (last and s >= 6):
                        if s in (2, 6):
                            pe.wait_ge(S("w_halved"), 4 * i + 2 * (s // 4 + 1) + 6)
                        up(i, s + 2)
                    down(i, s, last)

            pe.wait_ge(S(f"{m}_xh"), NQ)
            pe.wait_ge(S(f"{m}_xl"), 1)
            pe.wait_ge(S("w_halved"), 16 * r + 6)
            up(4 * r, 0, (0, 1))
            comb_tensor(pe, m, 0)
            up(4 * r, 0, (2, 3))
            comb_tensor(pe, m, 1)
            pe.wait_ge(S(f"{m}_xl"), 2)
            up(4 * r, 1)
            comb_bias(pe, m)
            pe.wait_ge(S(f"{m}_xl"), NQ)
            with pe.Fori(4 * r, 4 * r + 3) as i:
                body(i, False)
            body(4 * r + 3, True)
            for q in range(NQ):
                pe.wait_ge(S(f"{m}_y_odd" if q % 2 else f"{m}_y_even"), q // 2 + 1)
                for j in range(4):
                    t = 4 * q + j
                    ins = nc.tensor.transpose(ps[:, q, j * P:(j + 1) * P], XT[:, t * P:(t + 1) * P], ident[:, :])
                ins.then_inc(S(f"{m}_y_turned"), 1)

        def experts_scalar(act, m, r):
            def gelu(i, s, f):
                act.wait_ge(S("up_done"), 32 * i + 4 * s + f + 1)
                if f == 0:
                    act.wait_ge(S("halved"), 16 * i + 2 * s + 2)
                nc.scalar.activation(G[s % 2][:, f, :], ps[:, f, :], ACT.Gelu,
                                     bias=b1s[:, s // 4 % 2, f:f + 1]).then_inc(S("gelu_out"), 1)

            def high(i, s, half):
                act.wait_ge(S("weighted"), 16 + 16 * i + 2 * s + half + 1)
                act.wait_ge(S("down_done"), 8 * i + s + 7)
                c = slice(2 * half, 2 * half + 2)
                nc.scalar.activation(GH[s % 2][:, c, :], G[s % 2][:, c, :], ACT.Copy).then_inc(S("rounded"), 1)

            def body(i, last):
                for s in range(8):
                    more = not (last and s == 7)
                    if more:
                        if s in (3, 7):
                            act.wait_ge(S("b1_in"), 2 * i + s // 4 + 2)
                        gelu(i, s + 1, 0)
                        gelu(i, s + 1, 1)
                    high(i, s, 1)
                    if more:
                        gelu(i, s + 1, 2)
                        gelu(i, s + 1, 3)
                        high(i, s + 1, 0)

            act.wait_ge(S("b1_in"), 8 * r + 1)
            route_scalar(act, m, 1)
            for f in range(FC):
                gelu(4 * r, 0, f)
            comb_scalar(act, m, 1)
            high(4 * r, 0, 0)
            with act.Fori(4 * r, 4 * r + 3) as i:
                body(i, False)
            body(4 * r + 3, True)
            for q in (0, 2):
                act.wait_ge(S("down_done"), 8 + 32 * (r + 1) - 3 + q)
                nc.scalar.activation(XT[:, q * QW:(q + 1) * QW], ps[:, 4 + q, :], ACT.Copy).then_inc(S(f"{m}_y_even"), 1)

        def experts_vector(ve, m, r):
            def weigh(i, s, half):
                p, q = s // 4 % 2, s % 4
                ve.wait_ge(S("gelu_out"), 4 + 32 * i + 4 * s + 2 * half + 2)
                g = G[s % 2][:, 2 * half:2 * half + 2, :]
                nc.vector.tensor_tensor(g, g, CB[p][:, q * QW:(q + 1) * QW].unsqueeze(1).broadcast_to([P, 2, QW]),
                                        ALU.mult).then_inc(S("weighted"), 1)

            def low(i, s, half):
                ve.wait_ge(S("rounded"), 16 * i + 2 * s + half + 1)
                c = slice(2 * half, 2 * half + 2)
                nc.vector.tensor_tensor(GL[s % 2][:, c, :], G[s % 2][:, c, :], GH[s % 2][:, c, :],
                                        ALU.subtract).then_inc(S("halved"), 1)

            def body(i, last):
                for s in range(8):
                    more = not (last and s == 7)
                    if more:
                        if s in (0, 3, 7):
                            ve.wait_ge(S(f"cb_in{(s + 1) // 4 % 2}"), 16 * i + (32 if s == 7 else 16))
                        weigh(i, s + 1, 0)
                    low(i, s, 1)
                    if more:
                        weigh(i, s + 1, 1)
                        low(i, s + 1, 0)

            ve.wait_ge(S("cb_first_in"), 16 * r + 16)
            weigh(4 * r, 0, 0)
            weigh(4 * r, 0, 1)
            low(4 * r, 0, 0)
            with ve.Fori(4 * r, 4 * r + 3) as i:
                body(i, False)
            body(4 * r + 3, True)
            for q in (1, 3):
                ve.wait_ge(S("down_done"), 8 + 32 * (r + 1) - 3 + q)
                nc.vector.tensor_copy(XT[:, q * QW:(q + 1) * QW], ps[:, 4 + q, :]).then_inc(S(f"{m}_y_odd"), 1)
            for q in range(NQ):
                ve.wait_ge(S(f"{m}_y_turned"), q + 1)
                xq = X[:, 4 * q:4 * q + 4, :].rearrange("p t c -> p (t c)")
                nc.vector.tensor_tensor(xq, xq, ps[:, q, :], ALU.add).then_inc(S(f"{m}_x"), 1)

        def experts_gpsimd(g, m, r):
            def expert(i, p):
                hold(g, S("down_done"), 8 * i + 4 * p + 4)
                e = 2 * (i - 4 * r) + p
                nc.gpsimd.tensor_copy(b1s[:, p, :].unsqueeze(1), b1e[:, bass.ds(e, 1), :]).then_inc(S("b1_in"), 1)
                hold(g, S(f"w_in{p}"), 32 * i + 32)
                nc.gpsimd.tensor_copy(WH[p][:, :, :], WR[p][:, :, :]).then_inc(S("w_halved"), 1)
                hold(g, S("w_halved"), 4 * i + 2 * p + 5)
                nc.gpsimd.tensor_tensor(WL[p][:, :, :], WR[p][:, :, :], WH[p][:, :, :], ALU.subtract)\
                  .then_inc(S("w_halved"), 1)

            with g.Fori(4 * r, 4 * r + 4) as i:
                expert(i, 0)
                expert(i, 1)

        def experts_sync(sp, m, r, ready):
            def weights(i, p):
                hold(sp, S("w_halved"), 4 * i + 2 * p + 2)
                e = 2 * (i - 4 * r) + p
                sp.dma_start(WR[p][:, 0:1, :], dram["ffn_w1"][bass.ds(e, 1), :, :].rearrange("e p f -> p e f"))\
                  .then_inc(S(f"w_in{p}"), 16)
                sp.dma_start(WR[p][:, 1:2, :], dram["ffn_w2"][bass.ds(e, 1), :, :].rearrange("e p f -> p e f"))\
                  .then_inc(S(f"w_in{p}"), 16)

            def combines(i, p):
                hold(sp, S("weighted"), 16 * i + 8 * p + 8)
                e = 2 * (i - 4 * r) + p
                sp.dma_start(CB[p][:, :], cst[bass.ds(e, 1), :].broadcast_to([P, T])).then_inc(S(f"cb_in{p}"), 16)

            ready(sp)
            weights(4 * r, 0)
            weights(4 * r, 1)
            for part, (t0, t1) in enumerate(ROUTED):
                sp.wait_ge(S(f"{m}_combT_out"), part + 1)
                sp.dma_start(cst[:, t0 * P:t1 * P], combT[:, t0 * P:t1 * P]).then_inc(S("cst_out"), 16)
                sp.wait_ge(S("cst_out"), 32 * r + 16 * (part + 1))
                if part == 0:
                    sp.wait_ge(S("weighted"), 64 * r + 8)
                sp.dma_start(CB[0][:, t0 * P:t1 * P], cst[0:1, t0 * P:t1 * P].broadcast_to([P, (t1 - t0) * P]))\
                  .then_inc(S(("cb_first_in", "cb_in0")[part]), 16)
            combines(4 * r, 1)
            with sp.Fori(4 * r + 1, 4 * r + 4) as i:
                for p in range(2):
                    weights(i, p)
                    combines(i, p)

        @block.sync
        def _(sp):
            sp.dma_start(ident[:, :], dram["ident"]).then_inc(S("first_in"), 16)
            sp.dma_start(wqkva[:, :], dram["wqkva"]).then_inc(S("first_in"), 16)
            for name, dst in (("wpa", wpa), ("bpa", bpa),
                              ("wqkvb", wqkvb), ("colb", colb), ("bvb", bvb), ("bob", bob), ("b2b", b2b),
                              ("wob", wob), ("w1b", w1b), ("w2b", w2b), ("rw", rw), ("b1e", b1e), ("b2e", b2e),
                              ("tri", tri), ("causal", causal), ("identb", identb)):
                ap = dst[tuple(slice(None) for _ in dst.shape)]
                sp.dma_start(ap, dram[name]).then_inc(S("consts_in"), 16)
            def load(i, b):
                for j in range(2):
                    sp.dma_start(KA[b][KR * j:KR * j + KR, :, :], kst_q[i, j, :, :, b * N:(b + 1) * N])\
                      .then_inc(S(f"kq_in{b}"), 16)
                    sp.dma_start(QZ[b][KR * j:KR * j + KR, :, j, :], qst_q[i, j, :, :, b * N:(b + 1) * N])\
                      .then_inc(S(f"kq_in{b}"), 16)

            for b in range(B):
                stacks_sync(sp, "a", b, parts, qst, partk, kst, b * N)
                sp.wait_ge(S(f"aq_stacked{b}"), 16 * NR)
                sp.wait_ge(S(f"ak_stacked{b}"), 16 * NR)
                if b == 0:
                    sp.wait_ge(S("qz_clear"), 4)
                load(0, b)
            with sp.Fori(0, QUADS - 1) as i:
                for b in range(B):
                    hold(sp, S("exp_done"), 128 * i + 64 * b + 128)
                    load(i + 1, b)
            experts_sync(sp, "m0", 0, lambda sp: sp.wait_ge(S("x1"), NQ))
            sp.wait_ge(S("zero_ready"), 1)
            for b in range(B):
                sp.dma_start(kstb[:, :, b * PADN:b * PADN + BK].rearrange("h r t -> (h r) t")
                             .rearrange("(p g) t -> p g t", g=H * KR // P),
                             zer[:, 0:BK].unsqueeze(1).broadcast_to([P, H * KR // P, BK])).then_inc(S("b_pads"), 16)
            sp.wait_ge(S("b_pads"), 16 * B)

            def b_load(i, b, j):
                at = 2 * P * i + j * P
                sp.dma_start(QB[j][0:KR, :, :], qstb[:, :, bass.ds(at, P)].rearrange("h r t -> r h t"))\
                  .then_inc(S(f"b_qk_in{j}"), 16)
                sp.dma_start(KB[j][0:KR, :, :], kstb[:, :, bass.ds(at + BK * b, KW)].rearrange("h r t -> r h t"))\
                  .then_inc(S(f"b_qk_in{j}"), 16)

            def b_reload(i, b):
                for j in range(2):
                    hold(sp, S("b_scores"), 4 * i + 2 * j + 2)
                    b_load(i, b, j)

            def b_stack(b, first, end):
                stacks_sync(sp, "b", b, partsb, qstb, partkb, kstb, b * PADN + BK, first, end)

            def b_move(b):
                sp.wait_ge(S("b_v_out"), 2 * b + 2)
                sp.dma_start(V9[BK:P, 0, b * MT:(b + 1) * MT, :, :], V9[0:BK, 1, b * MT:(b + 1) * MT, :, :])\
                  .then_inc(S(f"bv_moved{b}"), 16)
                sp.dma_start(V9[0:BK, 0, b * MT + 1:(b + 1) * MT, :, :], V9[BK:P, 1, b * MT:(b + 1) * MT - 1, :, :])\
                  .then_inc(S(f"bv_moved{b}"), 16)

            b_stack(0, 0, 6)
            sp.wait_ge(S("bq_stacked0"), 16 * NR)
            sp.wait_ge(S("bk_stacked0"), 16 * NR)
            for j in range(2):
                b_load(0, 0, j)
            b_move(0)
            b_reload(1, 0)
            b_stack(1, 0, 2)
            b_reload(2, 0)
            b_stack(1, 2, 6)
            b_reload(3, 0)
            b_move(1)
            sp.wait_ge(S("bq_stacked1"), 16 * NR)
            sp.wait_ge(S("bk_stacked1"), 16 * NR)
            with sp.Fori(MT // 2, MT) as i:
                b_reload(i, 1)
            experts_sync(sp, "m1", 1, lambda sp: sp.wait_ge(S("x3"), NQ))
            sp.wait_ge(S("m1_x"), NQ)
            sp.dma_start(out.rearrange("b (t p) c -> p (b t) c", p=P), X[:, :, :]).then_inc(S("stored"), 16)
            sp.wait_ge(S("stored"), 16)

        @block.gpsimd
        def _(g):
            g.nop().then_inc(S("w_halved"), 4)
            g.nop().then_inc(S("msplit"), 4)
            nc.gpsimd.memset(mhalf[:, :], -0.5).then_inc(S("half_ready"), 1)
            g.wait_ge(S("half_ready"), 1)
            norm_gpsimd(g, "na")
            for b in range(B):
                nc.gpsimd.memset(QZ[b][:, :, :, :], 0.0).then_inc(S("qz_clear"), 1)
                nc.gpsimd.memset(KA[b][:, :, :], 1.0).then_inc(S("qz_clear"), 1)
                nc.gpsimd.memset(Vs[b][:, :, :, :], 0.0).then_inc(S("vs_set"), 1)
                g.wait_ge(S("vs_set"), 2 * b + 1)
                nc.gpsimd.memset(Vs[b][:, :, :, D:D + 1], 1.0).then_inc(S("vs_set"), 1)
            g.wait_ge(S("na_normed"), NT)
            g.wait_ge(S("consts_in"), 16 * 16)
            nc.gpsimd.tensor_tensor(X[:, :, :], X[:, :, :], bpa[:, :].unsqueeze(1).broadcast_to([P, NT, P]),
                                    ALU.add).then_inc(S("x_biased"), 1)
            g.wait_ge(S("vs_set"), 4)
            g.wait_ge(S("a_v_out"), NQ)

            def values(i, b):
                nc.gpsimd.tensor_copy(Vs[b][:, :, :, 0:D],
                                      Vn[:, bass.ds(B * i + b, 1), :, :].rearrange("p o m (h d) -> p (o m) h d", h=HQ))\
                  .then_inc(S("vs_in"), 1)

            def max_rows(i, b, nh, last=False):
                c = B * i + b
                hold(g, S("max_done"), ITEMS * c + turned_at(nh, last))
                q = S("msplit")
                k = 4 + 8 * c + 4 * nh
                nc.gpsimd.tensor_copy(mparts[nh][:, 0, :], neg[nh][:, :]).then_inc(q, 1)
                hold(g, q, k + 1)
                nc.gpsimd.tensor_tensor(nres[:, :], neg[nh][:, :], mparts[nh][:, 0, :], ALU.subtract).then_inc(q, 1)
                hold(g, q, k + 2)
                nc.gpsimd.tensor_copy(mparts[nh][:, 1, :], nres[:, :]).then_inc(q, 1)
                hold(g, q, k + 3)
                nc.gpsimd.tensor_tensor(mparts[nh][:, 2, :], nres[:, :], mparts[nh][:, 1, :], ALU.subtract).then_inc(q, 1)
                hold(g, q, k + 4)
                g.dma_start(mrow[b, nh].rearrange("s c n -> c s n"), mparts[nh][:, :, :]).then_inc(S(f"mrow_out{nh}"), 16)
                hold(g, S(f"mrow_out{nh}"), 16 * c + 16)
                g.dma_start(QZ[b][96:99, :, :, nh * 512:(nh + 1) * 512].rearrange("s a j n -> s (a j) n"),
                            mrow[b, nh].rearrange("s (h t) n -> s h (t n)", h=HQ)).then_inc(S(f"mrow_in{b}{nh}"), 16)

            max_rows(0, 0, 0)
            values(0, 0)
            values(0, 1)

            def follow(i, b, last):
                max_rows(i, b, 1, last and b == 1)
                if not (last and b == 1):
                    max_rows(i + b, 1 - b, 0)
                if not last:
                    hold(g, S("pv_done"), 2 + 32 * i + 16 * b + 16)
                    values(i + 1, b)

            with g.Fori(0, QUADS - 1) as i:
                for b in range(B):
                    follow(i, b, False)
            for b in range(B):
                follow(QUADS - 1, b, True)
            norm_gpsimd(g, "n0")
            experts_gpsimd(g, "m0", 0)
            norm_gpsimd(g, "nb")
            norm_gpsimd(g, "nb1")
            nc.gpsimd.memset(zer[:, :], 0.0).then_inc(S("zero_ready"), 1)
            for b in range(B):
                nc.gpsimd.memset(V9[0:BK, 0, b * MT, :, :], 0.0).then_inc(S("v9_zero"), 1)
            nc.gpsimd.memset(V9[:, 1, :, :, D:D + 1], 1.0).then_inc(S("v9_ones"), 1)
            for j in range(2):
                nc.gpsimd.memset(VWs[j][:, :, :, :], 0.0).then_inc(S("vws_zero"), 1)
            g.wait_ge(S("v9_zero"), B)
            for b in range(B):
                nc.gpsimd.memset(V9[0:BK, 0, b * MT, :, D:D + 1], 1.0).then_inc(S("v9_zero"), 1)
            g.wait_ge(S("nb1_normed"), NT)
            nc.gpsimd.tensor_tensor(XN[:, :, :], XN[:, :, :], bob[:, :].unsqueeze(1).broadcast_to([P, NT, P]),
                                    ALU.add).then_inc(S("xn_biased"), 1)
            g.wait_ge(S("v9_zero"), 2 * B)
            g.wait_ge(S("vws_zero"), 2)
            for b in range(B):
                g.wait_ge(S("b_v_out"), 2 * b + 2)
                g.wait_ge(S(f"bv_moved{b}"), 32)
                with g.Fori(b * MT // 2, (b + 1) * MT // 2) as i:
                    for j in range(2):
                        hold(g, S("b_pv"), 4 * i + 2 * j + 2)
                        nc.gpsimd.tensor_copy(VWs[j][:, :, :, 0:VW],
                                              V9[:, :, bass.ds(2 * i + j, 1), :, :].rearrange("p w t h c -> p (w t) h c"))\
                          .then_inc(S(f"b_v_in{j}"), 1)
            norm_gpsimd(g, "nb2")
            g.wait_ge(S("nb2_normed"), NT)
            nc.gpsimd.tensor_tensor(XN[:, :, :], XN[:, :, :], b2b[:, :].unsqueeze(1).broadcast_to([P, NT, P]),
                                    ALU.add).then_inc(S("xn_biased"), 1)
            g.wait_ge(S("xn_biased"), 2)
            nc.gpsimd.tensor_tensor(X[:, :, :], X[:, :, :], XN[:, :, :], ALU.add).then_inc(S("x_plus"), 1)
            norm_gpsimd(g, "n1")
            experts_gpsimd(g, "m1", 1)

        @block.scalar
        def _(act):
            for q in range(NQ):
                act.dma_start(X[:, 4 * q:4 * q + 4, :],
                              dram["x"].rearrange("b (t p) c -> p (b t) c", p=P)[:, 4 * q:4 * q + 4, :]).then_inc(S(f"x_in{q}"), 16)
            act.nop().then_inc(S("exp_done"), 64)
            act.nop().then_inc(S("gelu_out"), 4)
            turn_scalar(act, "na", XT)

            for q in range(NQ):
                act.wait_ge(S("a_qk"), 2 * q + 1)
                c = slice(q * QW, (q + 1) * QW)
                nc.scalar.activation(parts[:, 0, c], ps[:, q, :], ACT.Copy, scale=SCALE).then_inc(S("aq_hi"), 1)
                nc.scalar.activation(QF[:, c], ps[:, q, :], ACT.Copy, scale=SCALE).then_inc(S("a_q_out"), 1)
                act.wait_ge(S("a_qk"), 2 * q + 2)
                nc.scalar.activation(partk[:, 0, c], ps[:, 4 + q, :], ACT.Copy).then_inc(S("ak_hi"), 1)
                nc.scalar.activation(KF[:, c], ps[:, 4 + q, :], ACT.Copy).then_inc(S("a_k_out"), 1)
            for q in range(NQ):
                act.wait_ge(S("a_v"), q + 1)
                b, m = q // 2, q % 2
                for quad in range(QUADS):
                    ins = nc.scalar.activation(
                        Vn[:, B * quad + b, 4 * m:4 * m + 4, :],
                        ps[:, q, :].rearrange("p (m c) -> p m c", m=4)[:, :, 32 * quad:32 * quad + 32], ACT.Copy)
                ins.then_inc(S("a_v_out"), 1)

            def unit(i, b, u):
                for h in range(HQ):
                    k = 4 * u + h
                    act.wait_ge(S("s_full"), 128 * i + 64 * b + k + 1)
                    if h == 0:
                        act.wait_ge(S("pv_done"), 32 * i + 16 * b + u + 1)
                    nc.scalar.activation(EX[u % 2][:, h, :], ps[:, SB[k % 3], :], ACT.Exp).then_inc(S("exp_done"), 1)

            def output(i, b, nh):
                act.wait_ge(S("pv_done"), 2 + 32 * i + 16 * b + 8 * nh + 8)
                nc.scalar.activation(OT[:, bass.ds(i, 1), b * N + nh * 512:b * N + (nh + 1) * 512],
                                     ps[:, OB, :].unsqueeze(1), ACT.Copy).then_inc(S("o_out"), 1)

            def combination(i, b, more):
                for u in range(1, UNITS):
                    unit(i, b, u)
                    if u == MT:
                        output(i, b, 0)
                if more:
                    unit(i + b, 1 - b, 0)
                output(i, b, 1)

            unit(0, 0, 0)
            with act.Fori(0, QUADS - 1) as i:
                combination(i, 0, True)
                combination(i, 1, True)
            combination(QUADS - 1, 0, True)
            combination(QUADS - 1, 1, False)

            head_back_scalar(act, 0, 2)
            expert_in_scalar(act, "m0")
            route_scalar(act, "m0", 0)
            comb_scalar(act, "m0", 0)
            experts_scalar(act, "m0", 0)
            turn_scalar(act, "b1", XT, colb[:, LN1G:LN1G + 1], colb[:, LN1B:LN1B + 1])
            for q in range(NQ):
                c = slice(q * QW, (q + 1) * QW)
                act.wait_ge(S("b_qk"), 2 * q + 2)
                nc.scalar.activation(partkb[:, 0, c], ps[:, 4 + q, :], ACT.Identity,
                                     bias=colb[:, BKC:BKC + 1]).then_inc(S("bk_hi"), 1)
                nc.scalar.activation(KFb[:, c], ps[:, 4 + q, :], ACT.Identity,
                                     bias=colb[:, BKC:BKC + 1]).then_inc(S("b_k_out"), 1)
                act.wait_ge(S("b_q_out"), q + 1)
                nc.scalar.activation(partsb[:, 0, c], QFb[:, c], ACT.Copy).then_inc(S("bq_hi"), 1)

            def b_exp(u, j):
                act.wait_ge(S("b_shifted"), u + 1)
                nc.scalar.activation(PB[j], PB[j], ACT.Exp).then_inc(S("b_exp"), 1)

            def b_output(u, tile, j):
                act.wait_ge(S("b_pv"), u + 1 + 4)
                nc.scalar.activation(OTb[:, 2 * j:2 * j + 2, bass.ds(P * tile, P)],
                                     ps[:, 4 + 2 * j, 0:2 * P].rearrange("p (q n) -> p q n", q=2), ACT.Copy)\
                  .then_inc(S("b_out"), 1)

            def b_scalar(i, first=False, last=False):
                for k in range(4):
                    u, j = 4 * i + k, k % 2
                    if not (last and k == 3):
                        b_exp(u + 1, 1 - j)
                    act.wait_ge(S("b_pturned"), u + 1)
                    act.wait_ge(S("b_pv"), u + 4 - 1)
                    nc.scalar.activation(PT[j], ps[:, 4 + 2 * j:6 + 2 * j, :].rearrange("p a (h n) -> p (a h) n", h=4),
                                         ACT.Copy).then_inc(S("b_pt"), 1)
                    if not (first and k == 0):
                        b_output(u - 1, 2 * i + (k - 1) // 2, 1 - j)

            b_exp(0, 0)
            b_scalar(0, first=True)
            with act.Fori(1, BU // 4 - 1) as i:
                b_scalar(i)
            b_scalar(BU // 4 - 1, last=True)
            b_output(BU - 1, NT - 1, 1)
            head_back_scalar(act, 1)
            turn_scalar(act, "b2", XT, colb[:, LN2G:LN2G + 1], colb[:, LN2B:LN2B + 1])
            for s in range(NQ):
                for f in range(FC):
                    act.wait_ge(S("mlp_up"), 4 * s + f + 1)
                    if f == 0 and s >= 2:
                        act.wait_ge(S("mlp_down"), s - 1)
                    nc.scalar.activation(Gb[s % 2][:, f, :], ps[:, f, :], ACT.Gelu,
                                         bias=colb[:, B1C + f:B1C + f + 1]).then_inc(S("mlp_gelu"), 1)
            expert_in_scalar(act, "m1")
            route_scalar(act, "m1", 0)
            comb_scalar(act, "m1", 0)
            experts_scalar(act, "m1", 1)

        @block.vector
        def _(ve):
            ve.nop().then_inc(S("weighted"), 16)
            ve.nop().then_inc(S("halved"), 4)
            norm_vector(ve, "na", X, XN, lambda q: (S(f"x_in{q}"), 16))
            turn_vector(ve, "na", XT)
            for b in range(B):
                ve.wait_ge(S("a_q_out"), 2 * b + 2)
                split_vector(ve, "aq", QF, parts, b)
                ve.wait_ge(S("a_k_out"), 2 * b + 2)
                split_vector(ve, "ak", KF, partk, b)

            def maxima(i, b, last=False):
                c = B * i + b
                first = isinstance(c, int) and c == 0
                for k in range(ITEMS):
                    item, ahead = slot_item(k, first, last)
                    ve.wait_ge(S("max_full"), ITEMS * c + k + 1)
                    nh = item[1]
                    if item[0] == "max":
                        _, _, h, nt = item
                        nc.vector.tensor_reduce(mx[nh][:, 4 * h + nt:4 * h + nt + 1],
                                                ps[:, MB[k % 2]:MB[k % 2] + 2, :].rearrange("p a n -> p (a n)"), AX, ALU.max)\
                          .then_inc(S("max_done"), 1)
                    else:
                        if not first:
                            ve.wait_ge(S("msplit"), 8 * c + 8 * ahead + 4 * nh)
                        nc.vector.tensor_scalar(neg[nh][:, :], ps[0:16, MB[k % 2], 0:P], -1.0, None, ALU.mult)\
                          .then_inc(S("max_done"), 1)

            maxima(0, 0)
            with ve.Fori(0, QUADS - 1) as i:
                maxima(i, 1)
                maxima(i + 1, 0)
            maxima(QUADS - 1, 1, True)
            def early_back(q):
                ve.wait_ge(S("head_back"), q + 1)
                nc.vector.tensor_copy(XT[:, q * QW:(q + 1) * QW], ps[:, 6, :]).then_inc(S("head_xt"), 1)

            def a_add(q, bank):
                ve.wait_ge(S("head_proj"), q + 1)
                xq = X[:, 4 * q:4 * q + 4, :].rearrange("p t c -> p (t c)")
                nc.vector.tensor_tensor(xq, xq, ps[:, bank, :], ALU.add).then_inc(S("x1"), 1)

            ve.wait_ge(S("x_biased"), 1)
            for t in range(5):
                head_norm(ve, 0, t, 4 + t % 2)
            early_back(0)
            head_norm(ve, 0, 5, 5)
            a_add(0, 7)
            head_norm(ve, 0, 6, 4)
            head_norm(ve, 0, 7, 5)
            early_back(1)
            a_add(1, 7)
            for q in range(2):
                ve.wait_ge(S("x1"), q + 1)
                norm_moments(ve, "n0", X, q)
            head_norm_vector(ve, 0, 8)
            for q in range(2, NQ):
                a_add(q, 6 + q % 2)
            for q in range(2, NQ):
                ve.wait_ge(S("x1"), q + 1)
                norm_moments(ve, "n0", X, q)
            norm_apply(ve, "n0", X, XN)
            route_vector(ve, "m0")
            experts_vector(ve, "m0", 0)
            norm_vector(ve, "nb", X, XN, lambda q: (S("m0_x"), q + 1))
            ve.wait_ge(S("nb_normed"), NT)
            norm_vector(ve, "nb1", XN, HN)
            turn_vector(ve, "b1", XT, colb[:, LN1G:LN1G + 1], colb[:, LN1B:LN1B + 1])
            for q in range(NQ):
                ve.wait_ge(S("b_qk"), 2 * q + 1)
                nc.vector.tensor_scalar(QFb[:, q * QW:(q + 1) * QW], ps[:, q, :], colb[:, BQ:BQ + 1], SCALE,
                                        ALU.add, ALU.mult).then_inc(S("b_q_out"), 1)
            for b in range(B):
                split_vector(ve, "bq", QFb, partsb, b)
                ve.wait_ge(S("b_k_out"), 2 * b + 2)
                split_vector(ve, "bk", KFb, partkb, b)
                ve.wait_ge(S("v9_ones"), 1)
                for q in range(2 * b, 2 * b + 2):
                    ve.wait_ge(S("b_v"), q + 1)
                    for j in range(4):
                        t = 4 * q + j
                        ins = nc.vector.tensor_tensor(V9[:, 1, t, :, 0:D],
                                                      ps[:, q, j * P:(j + 1) * P].rearrange("p (h d) -> p h d", h=H),
                                                      bvb[:, :].rearrange("p (h d) -> p h d", h=H), ALU.add)
                    ins.then_inc(S("b_v_out"), 1)

            def b_shift(u, j):
                ve.wait_ge(S("b_scores"), u + 1 + 4)
                sc = ps[:, 2 * j:2 * j + 2, :].rearrange("p a (h n) -> p (a h) n", h=4)
                nc.vector.tensor_reduce(mxb[:, j, :], sc, AX, ALU.max).then_inc(S("b_max"), 1)
                ve.wait_ge(S("b_max"), u + 1)
                if not (isinstance(u, int) and u < 2):
                    ve.wait_ge(S("b_pturned"), u - 1)
                nc.vector.tensor_tensor(PB[j], sc, mxb[:, j, :].unsqueeze(2).broadcast_to([P, HH, P]), ALU.subtract)\
                  .then_inc(S("b_shifted"), 1)

            b_shift(0, 0)
            b_shift(1, 1)
            with ve.Fori(0, BU // 4 - 1) as i:
                for k in range(4):
                    b_shift(4 * i + k + 2, k % 2)
            b_shift(BU - 2, 0)
            b_shift(BU - 1, 1)
            head_norm_vector(ve, 1)
            ve.wait_ge(S("xn_biased"), 1)
            for q in range(NQ):
                ve.wait_ge(S("head_proj"), NQ + q + 1)
                xq = XN[:, 4 * q:4 * q + 4, :].rearrange("p t c -> p (t c)")
                nc.vector.tensor_tensor(xq, xq, ps[:, 6 + q % 2, :], ALU.add).then_inc(S("xb1"), 1)
            norm_vector(ve, "nb2", XN, HN, lambda q: (S("xb1"), q + 1))
            turn_vector(ve, "b2", XT, colb[:, LN2G:LN2G + 1], colb[:, LN2B:LN2B + 1])
            ve.wait_ge(S("x_plus"), 1)
            for s in range(NQ):
                ve.wait_ge(S("mlp_down"), s + 1)
                xq = X[:, 4 * s:4 * s + 4, :].rearrange("p t c -> p (t c)")
                nc.vector.tensor_tensor(xq, xq, ps[:, 4 + s % 2, :], ALU.add).then_inc(S("x3"), 1)
            norm_vector(ve, "n1", X, XN, lambda q: (S("x3"), q + 1))
            route_vector(ve, "m1")
            experts_vector(ve, "m1", 1)

        @block.tensor
        def _(pe):
            pe.nop().then_inc(S("pv_done"), 2)
            pe.nop().then_inc(S("down_done"), 8)
            pe.wait_ge(S("first_in"), 32)
            turn_tensor(pe, "na", XN, S("na_normed"))
            qk_tensor(pe, "a", wqkva, "na")
            v_tensor(pe, "a", wqkva)

            def max_item(i, b, k, last=False):
                c = B * i + b
                first = isinstance(c, int) and c == 0
                item, ahead = slot_item(k, first, last)
                if not (first and k < 2):
                    pe.wait_ge(S("max_done"), ITEMS * c + k - (0 if last and k == ITEMS - 1 else 1))
                if item[0] == "max":
                    _, nh, h, nt = item
                    n0 = 512 * nh + P * nt
                    bb = (b + ahead) % B
                    for mh in range(2):
                        ins = nc.tensor.matmul(ps[:, MB[k % 2] + mh, :], QZ[bb][0:96, h // 2, h % 2, n0:n0 + P],
                                               KA[bb][0:96, h // 2, 512 * mh:512 * mh + 512], start=True, stop=True)
                    ins.then_inc(S("max_full"), 1)
                else:
                    nc.tensor.transpose(ps[0:16, MB[k % 2], 0:P], mx[item[1]][:, :], ident[:, :]).then_inc(S("max_full"), 1)

            def weigh(i, b, u):
                nh, mt = u // MT, u % MT
                pe.wait_ge(S("exp_done"), 64 + 128 * i + 64 * b + 4 * u + 4)
                if mt == 0:
                    if u == 0:
                        pe.wait_ge(S("vs_in"), 2 * i + b + 1)
                    pe.wait_ge(S("o_out"), 4 * i + 2 * b + nh + 1)
                for h in range(HQ):
                    last = nc.tensor.matmul(ps[32 * h:32 * h + 32, OB, :], Vs[b][:, mt, h, :], EX[u % 2][:, h, :],
                                            start=(mt == 0), stop=(mt == MT - 1))
                last.then_inc(S("pv_done"), 1)

            def scores(i, b, u, more):
                nh, mt = u // MT, u % MT
                if u < NEXT:
                    at = ITEMS - CARRY + sum(PLAN[:u])
                    todo = [(i, b, k, not more) for k in range(at, at + PLAN[u])]
                else:
                    at = sum(PLAN[NEXT:u])
                    todo = [(i + b, 1 - b, k) for k in range(at, at + PLAN[u])] if more else []
                if mt == 0:
                    pe.wait_ge(S(f"mrow_in{b}{nh}"), 16 * i + 16)
                if u == NEXT - 1 and more:
                    pe.wait_ge(S(f"kq_in{1 - b}"), 64 * (i + b) + 64)
                for h in range(HQ):
                    k = 4 * u + h
                    back = 3 if k >= 3 else {0: 1, 1: 4, 2: 4}[k]
                    pe.wait_ge(S("exp_done"), 64 + 128 * i + 64 * b + k - back + 1)
                    nc.tensor.matmul(ps[:, SB[k % 3], :], KA[b][0:99, h // 2, mt * P:(mt + 1) * P],
                                     QZ[b][0:99, h // 2, h % 2, 512 * nh:512 * nh + 512],
                                     start=True, stop=True).then_inc(S("s_full"), 1)
                    if todo and (h in (0, 2) or len(todo) > (3 - h) // 2):
                        max_item(*todo.pop(0))

            def combination(i, b, more, beside=()):
                for u in range(1, UNITS):
                    scores(i, b, u, more)
                    for v, work in beside:
                        if u == v:
                            work()
                    weigh(i, b, u - 1)
                if more:
                    scores(i + b, 1 - b, 0, True)
                weigh(i, b, UNITS - 1)

            pe.nop().then_inc(S("o_out"), 1)
            pe.wait_ge(S("consts_in"), 16 * 16)
            pe.wait_ge(S("kq_in0"), 64)
            pe.wait_ge(S("a_v_out"), NQ)
            pe.wait_ge(S("a_k_out"), NQ)
            for k in range(ITEMS - CARRY):
                max_item(0, 0, k)
            scores(0, 0, 0, True)
            with pe.Fori(0, QUADS - 1) as i:
                combination(i, 0, True)
                combination(i, 1, True)
            combination(QUADS - 1, 0, True)

            def early_turn(t):
                if t == 0:
                    pe.wait_ge(S("o_out"), 1 + 4 * QUADS - 2)
                    pe.wait_ge(S("max_done"), ITEMS * B * QUADS)
                if t >= 2:
                    pe.wait_ge(S("o_normed"), t - 1)
                head_turn(pe, OT, t, 4 + t % 2)

            combination(QUADS - 1, 1, False, (
                (5, lambda: early_turn(0)), (5, lambda: early_turn(1)), (6, lambda: early_turn(2)),
                (7, lambda: early_turn(3)), (8, lambda: early_turn(4)), (8, lambda: head_turn_back(pe, 0, 0, 6, 1)),
                (9, lambda: early_turn(5)), (10, lambda: head_project(pe, 0, 0, wpa, 7)),
                (10, lambda: early_turn(6)), (11, lambda: early_turn(7)),
                (13, lambda: head_turn_back(pe, 0, 1, 6, 1)), (15, lambda: head_project(pe, 0, 1, wpa, 7, (S("x1"), 1)))))

            pe.wait_ge(S("o_out"), 1 + 4 * QUADS)
            head_project_tensor(pe, 0, OT, wpa, S("x1"), 2)
            route_tensor(pe, "m0", XN, S("n0_normed"))
            experts_tensor(pe, "m0", 0)
            turn_tensor(pe, "b1", HN, S("nb1_normed"))
            qk_tensor(pe, "b", wqkvb, "b1")
            v_tensor(pe, "b", wqkvb)
            pe.wait_ge(S("b_v_out"), NQ)
            pe.wait_ge(S("b_k_out"), NQ)
            pe.nop().then_inc(S("b_scores"), 4)
            pe.nop().then_inc(S("b_pv"), 4)
            pe.nop().then_inc(S("b_out"), 2)

            def b_scores(u, tile, half, j):
                if not (isinstance(u, int) and u < 2):
                    pe.wait_ge(S("b_shifted"), u - 1)
                for bank in (2 * j, 2 * j + 1):
                    nc.tensor.matmul(ps[:, bank, :].rearrange("p (h n) -> p h n", h=4)[:, :, BK:P], identb[:, :],
                                     causal[:, BK:P].unsqueeze(1).broadcast_to([P, 4, BK]), start=True, stop=True,
                                     skip_group_check=True)
                    for hh in range(4):
                        h = HH * half + 4 * (bank - 2 * j) + hh
                        for w in range(2):
                            last = nc.tensor.matmul(ps[BK * w:BK * w + BK, bank, hh * P:(hh + 1) * P],
                                                    QB[tile][0:KR, h, BK * w:BK * w + BK],
                                                    KB[tile][0:KR, h, BK * w:BK * w + P],
                                                    start=False, stop=True, skip_group_check=True)
                last.then_inc(S("b_scores"), 1)

            def b_values(u, k, i):
                j, tile, half = k % 2, k // 2, k % 2
                pe.wait_ge(S("b_pt"), u + 1)
                if half == 0:
                    pe.wait_ge(S(f"b_v_in{tile}"), i + 1)
                for hh in range(HH):
                    for w in range(2):
                        n0 = P * (hh // 4) + BK * w
                        ins = nc.tensor.matmul(ps[32 * (hh % 4):32 * (hh % 4) + 32, 4 + 2 * j, n0:n0 + BK],
                                               VWs[tile][:, w, HH * half + hh, :], PT[j][:, hh, BK * w:BK * w + BK],
                                               start=True, stop=True, skip_group_check=True)
                ins.then_inc(S("b_pv"), 1)

            def b_tensor(i, first=False, last=False):
                for k in range(4):
                    u, j, tile, half = 4 * i + k, k % 2, k // 2, k % 2
                    if not (last and k >= 2):
                        if half == 0:
                            pe.wait_ge(S(f"b_qk_in{1 - tile}"), 32 * i + 32 + 32 * tile)
                        b_scores(u + 2, 1 - tile, half, j)
                    pe.wait_ge(S("b_exp"), u + 1)
                    pe.wait_ge(S("b_out"), u + 1)
                    for hh in range(HH):
                        ins = nc.tensor.transpose(ps[:, 4 + 2 * j + hh // 4, (hh % 4) * P:(hh % 4 + 1) * P],
                                                  PB[j][:, hh, :], ident[:, :])
                    ins.then_inc(S("b_pturned"), 1)
                    if not (first and k == 0):
                        b_values(u - 1, (k - 1) % 4, i)

            pe.wait_ge(S("b_qk_in0"), 32)
            b_scores(0, 0, 0, 0)
            b_scores(1, 0, 1, 1)
            b_tensor(0, first=True)
            with pe.Fori(1, BU // 4 - 1) as i:
                b_tensor(i)
            b_tensor(BU // 4 - 1, last=True)
            b_values(BU - 1, 3, BU // 4 - 1)
            pe.wait_ge(S("b_out"), 2 + BU)
            head_project_tensor(pe, 1, OTb, wob, S("xb1"))
            turn_tensor(pe, "b2", HN, S("nb2_normed"))
            for q in range(NQ):
                turned_wait(pe, "b2", q)

            def mlp_down(s):
                pe.wait_ge(S("mlp_gelu"), 4 * s + 4)
                if s >= 2:
                    pe.wait_ge(S("x3"), s - 1)
                else:
                    pe.wait_ge(S("xb1"), NQ)
                for j in range(4):
                    for f in range(FC):
                        last = nc.tensor.matmul(ps[:, 4 + s % 2, j * P:(j + 1) * P], Gb[s % 2][:, f, j * P:(j + 1) * P],
                                                w2b[:, f, :], start=(f == 0), stop=(f == FC - 1))
                last.then_inc(S("mlp_down"), 1)

            for s in range(NQ):
                for f in range(FC):
                    if s:
                        pe.wait_ge(S("mlp_gelu"), 4 * s - 3 + f)
                    nc.tensor.matmul(ps[:, f, :], w1b[:, f * P:(f + 1) * P], XT[:, s * QW:(s + 1) * QW],
                                     start=True, stop=True).then_inc(S("mlp_up"), 1)
                if s:
                    mlp_down(s - 1)
            mlp_down(NQ - 1)
            route_tensor(pe, "m1", XN, S("n1_normed"))
            experts_tensor(pe, "m1", 1)


def kernel(**inputs):
    import numpy as np
    import concourse.bacc as bacc
    from concourse.bass_utils import run_bass_kernel_spmd

    a = {k: np.ascontiguousarray(v) for k, v in inputs.items()}
    import ml_dtypes
    f32 = np.float32

    def blockdiag(w):
        g, ci, co = w.shape
        full = np.zeros((g * ci, g * co), f32)
        for k in range(g):
            full[k * ci:(k + 1) * ci, k * co:(k + 1) * co] = w[k]
        return full

    def rows(v):
        return np.ascontiguousarray(np.broadcast_to(v, (P, v.shape[0])))

    bq = a["L0_attn_b_b_qkv"]
    cols = [a["L0_attn_b_ln1_g"], a["L0_attn_b_ln1_b"], a["L0_attn_b_ln2_g"], a["L0_attn_b_ln2_b"],
            bq[0:P], bq[P:2 * P]] + [a["L0_attn_b_b1"][f * P:(f + 1) * P] for f in range(FC)]
    cols += [np.zeros(P, f32)] * (12 - len(cols))
    causal = np.zeros((P, P), f32)
    for i in range(P):
        causal[i, BK + i % BK + 1:] = -1e30
    arrays = {
        "x": a["L0_attn_a_x"],
        "wqkva": blockdiag(a["L0_attn_a_w_qkv"]), "wpa": blockdiag(a["L0_attn_a_w_proj"]), "bpa": rows(a["L0_attn_a_b_proj"]),
        "ident": np.eye(P, dtype=f32), "identb": np.eye(P, dtype=ml_dtypes.bfloat16),
        "causal": causal.astype(ml_dtypes.bfloat16),
        "tri": np.ascontiguousarray(np.broadcast_to(np.tril(np.ones((E, E), ml_dtypes.bfloat16), -1), (P, E, E))),
        "wqkvb": a["L0_attn_b_w_qkv"], "colb": np.ascontiguousarray(np.stack(cols, axis=1)),
        "bvb": rows(bq[2 * P:3 * P]), "bob": rows(a["L0_attn_b_b_out"]), "b2b": rows(a["L0_attn_b_b2"]),
        "wob": a["L0_attn_b_w_out"], "w1b": a["L0_attn_b_w1"],
        "w2b": np.ascontiguousarray(a["L0_attn_b_w2"].reshape(FC, P, P).transpose(1, 0, 2)),
        "rw": np.ascontiguousarray(a["L0_ffn_router_w"].T),
        "b1e": np.ascontiguousarray(a["L0_ffn_b1"].reshape(E, FC, P).transpose(2, 0, 1)),
        "b2e": a["L0_ffn_b2"],
        "ffn_w1": np.ascontiguousarray(a["L0_ffn_w1"].transpose(0, 2, 1)),
        "ffn_w2": np.ascontiguousarray(a["L0_ffn_w2"].reshape(E, P, FC, P).transpose(0, 3, 2, 1)).reshape(E, P, FF),
    }
    nc = bacc.Bacc("TRN2", target_bir_lowering=False, num_devices=1)
    dram = {k: nc.dram_tensor(f"in_{k}", v.shape, mybir.dt.from_np(v.dtype), kind="ExternalInput").ap()
            for k, v in arrays.items()}
    out = nc.dram_tensor("out", (B, N, P), F32, kind="ExternalOutput").ap()
    build(nc, dram, out)
    r = run_bass_kernel_spmd(nc, [{f"in_{k}": v for k, v in arrays.items()}], core_ids=[0])
    return r.results[0]["out"]
```
